# Optimizing a Trainium2 kernel written in Bass

```python
import numpy as np
import jax
import jax.numpy as jnp

def _softmax(x, axis=-1):
    return jax.nn.softmax(x, axis=axis)

def _gelu(x):
    return jax.nn.gelu(x, approximate=True)

def _silu(x):
    return jax.nn.silu(x)

def _sigmoid(x):
    return jax.nn.sigmoid(x)

def _layernorm(x, axis=-1, eps=1e-05):
    m = jnp.mean(x, axis=axis, keepdims=True)
    v = jnp.var(x, axis=axis, keepdims=True)
    return (x - m) / jnp.sqrt(v + eps)

def _scatter_add(tgt, idx, src, axis=0):
    return tgt.at[idx].add(src)

def _segment_sum(src, seg, n):
    return jax.ops.segment_sum(src, seg, n)
kernel_name = 'mk_hybrid_d1_jaxref_r8_7d6f32'

def setup_inputs(seed: int=0):
    np.random.seed(seed)
    _w = jnp.asarray

    def _L0_attn_a_setup():
        import jax, jax.numpy as jnp
        import numpy as np
        from jax import lax
        D_MODEL = 128
        EXPAND = 2
        D_INNER = EXPAND * D_MODEL
        D_STATE = 16
        D_CONV = 4
        DT_RANK = (D_MODEL + 15) // 16
        BATCH, SEQ = (2, 128)

        def _layernorm(x, gamma, beta, eps=1e-05):
            mu = jnp.mean(x, axis=-1, keepdims=True)
            var = jnp.mean(jnp.square(x - mu), axis=-1, keepdims=True)
            return (x - mu) * lax.rsqrt(var + eps) * gamma + beta

        def _mamba_block(x, gamma, beta, W_in, W_conv, b_conv, W_x, W_dt, b_dt, A_log, Dskip, W_out):
            h = _layernorm(x, gamma, beta)
            xz = h @ W_in
            xi, z = jnp.split(xz, 2, axis=-1)
            xt = xi.transpose(0, 2, 1)
            conv = lax.conv_general_dilated(xt, W_conv[:, None, :], window_strides=(1,), padding=[(D_CONV - 1, 0)], feature_group_count=D_INNER)
            u = jax.nn.silu(conv + b_conv[None, :, None]).transpose(0, 2, 1)
            x_dbl = u @ W_x
            dt_r = x_dbl[..., :DT_RANK]
            Bm = x_dbl[..., DT_RANK:DT_RANK + D_STATE]
            Cm = x_dbl[..., DT_RANK + D_STATE:]
            dt = jax.nn.softplus(dt_r @ W_dt + b_dt)
            A = -jnp.exp(A_log)

            def step(hstate, inp):
                dt_s, B_s, C_s, u_s = inp
                dA = jnp.exp(dt_s[..., None] * A)
                hstate = dA * hstate + (dt_s * u_s)[..., None] * B_s[:, None, :]
                y = jnp.einsum('bdn,bn->bd', hstate, C_s)
                return (hstate, y)
            h0 = jnp.zeros((x.shape[0], D_INNER, D_STATE), x.dtype)
            _, ys = lax.scan(step, h0, (dt.transpose(1, 0, 2), Bm.transpose(1, 0, 2), Cm.transpose(1, 0, 2), u.transpose(1, 0, 2)))
            y = ys.transpose(1, 0, 2) + u * Dskip
            y = y * jax.nn.silu(z)
            return x + y @ W_out
        key = jax.random.key(seed)
        ks = jax.random.split(key, 10)
        g = lambda k, shape, sc: jax.random.normal(k, shape, jnp.float32) * sc
        A_log = jnp.log(jnp.broadcast_to(jnp.arange(1, D_STATE + 1, dtype=jnp.float32), (D_INNER, D_STATE)))
        return {'x': jax.random.normal(ks[0], (BATCH, SEQ, D_MODEL), jnp.float32), 'gamma': jnp.ones((D_MODEL,), jnp.float32), 'beta': jnp.zeros((D_MODEL,), jnp.float32), 'W_in': g(ks[1], (D_MODEL, 2 * D_INNER), 0.02), 'W_conv': g(ks[2], (D_INNER, D_CONV), 0.1), 'b_conv': jnp.zeros((D_INNER,), jnp.float32), 'W_x': g(ks[3], (D_INNER, DT_RANK + 2 * D_STATE), 0.02), 'W_dt': g(ks[4], (DT_RANK, D_INNER), 0.1), 'b_dt': g(ks[5], (D_INNER,), 0.1), 'A_log': A_log, 'Dskip': jnp.ones((D_INNER,), jnp.float32), 'W_out': g(ks[6], (D_INNER, D_MODEL), 0.02)}
    _L0_attn_a_in = _L0_attn_a_setup()

    def _L0_attn_b_setup():
        import jax, jax.numpy as jnp
        import numpy as np
        HID = 128
        EXP = 512

        def _min_gru(x_in, Wz, bz, Wh, bh):
            z = jax.nn.sigmoid(jnp.einsum('bse,ef->bsf', x_in, Wz) + bz)
            h_tilde = jnp.einsum('bse,ef->bsf', x_in, Wh) + bh
            a = 1.0 - z
            b = z * h_tilde

            def combine(c1, c2):
                a1, b1 = c1
                a2, b2 = c2
                return (a2 * a1, a2 * b1 + b2)
            _, h = jax.lax.associative_scan(combine, (a, b), axis=1)
            return h
        key = jax.random.key(seed)
        ks = jax.random.split(key, 11)
        s = lambda fan_in: 1.0 / np.sqrt(fan_in)
        return {'x': jax.random.normal(ks[0], (4, 256, HID), dtype=jnp.float32), 'W1': jax.random.uniform(ks[1], (HID, EXP), jnp.float32, -s(HID), s(HID)), 'b1': jax.random.uniform(ks[2], (EXP,), jnp.float32, -s(HID), s(HID)), 'W2': jax.random.uniform(ks[3], (HID, EXP), jnp.float32, -s(HID), s(HID)), 'b2': jax.random.uniform(ks[4], (EXP,), jnp.float32, -s(HID), s(HID)), 'Wz': jax.random.uniform(ks[5], (EXP, EXP), jnp.float32, -s(EXP), s(EXP)), 'bz': jax.random.uniform(ks[6], (EXP,), jnp.float32, -s(EXP), s(EXP)), 'Wh': jax.random.uniform(ks[7], (EXP, EXP), jnp.float32, -s(EXP), s(EXP)), 'bh': jax.random.uniform(ks[8], (EXP,), jnp.float32, -s(EXP), s(EXP)), 'Wo': jax.random.uniform(ks[9], (EXP, HID), jnp.float32, -s(EXP), s(EXP)), 'bo': jax.random.uniform(ks[10], (HID,), jnp.float32, -s(EXP), s(EXP))}
    _L0_attn_b_in = _L0_attn_b_setup()

    def _L0_ffn_setup():
        import jax, jax.numpy as jnp
        import numpy as np
        EPS = 1e-08

        def _ternary_linear(x, w):
            alpha = jnp.mean(jnp.abs(w))
            w_t = jnp.sign(w) * (jnp.abs(w) > 0.5 * alpha).astype(w.dtype)
            w_q = w + jax.lax.stop_gradient(w_t - w)
            d = x.shape[-1]
            rms = jnp.sqrt(jnp.sum(x * x, axis=-1, keepdims=True)) / jnp.sqrt(jnp.asarray(d, x.dtype))
            x_norm = x / (rms + EPS)
            return jnp.einsum('bsd,fd->bsf', x_norm, w_q)
        key = jax.random.key(seed)
        k1, k2, k3 = jax.random.split(key, 3)
        d_model, d_ff = (128, 512)
        B, S = (4, 512)
        x = jax.random.normal(k1, (B, S, d_model), dtype=jnp.float32)
        w_up = jax.random.normal(k2, (d_ff, d_model), dtype=jnp.float32) * 0.02
        w_down = jax.random.normal(k3, (d_model, d_ff), dtype=jnp.float32) * 0.02
        return {'x': x, 'w_up': w_up, 'w_down': w_down}
    _L0_ffn_in = _L0_ffn_setup()
    _d = {'L0_attn_a_x': _L0_attn_a_in['x'], 'L0_attn_a_gamma': _L0_attn_a_in['gamma'], 'L0_attn_a_beta': _L0_attn_a_in['beta'], 'L0_attn_a_W_in': _L0_attn_a_in['W_in'], 'L0_attn_a_W_conv': _L0_attn_a_in['W_conv'], 'L0_attn_a_b_conv': _L0_attn_a_in['b_conv'], 'L0_attn_a_W_x': _L0_attn_a_in['W_x'], 'L0_attn_a_W_dt': _L0_attn_a_in['W_dt'], 'L0_attn_a_b_dt': _L0_attn_a_in['b_dt'], 'L0_attn_a_A_log': _L0_attn_a_in['A_log'], 'L0_attn_a_Dskip': _L0_attn_a_in['Dskip'], 'L0_attn_a_W_out': _L0_attn_a_in['W_out'], 'L0_attn_b_W1': _L0_attn_b_in['W1'], 'L0_attn_b_b1': _L0_attn_b_in['b1'], 'L0_attn_b_W2': _L0_attn_b_in['W2'], 'L0_attn_b_b2': _L0_attn_b_in['b2'], 'L0_attn_b_Wz': _L0_attn_b_in['Wz'], 'L0_attn_b_bz': _L0_attn_b_in['bz'], 'L0_attn_b_Wh': _L0_attn_b_in['Wh'], 'L0_attn_b_bh': _L0_attn_b_in['bh'], 'L0_attn_b_Wo': _L0_attn_b_in['Wo'], 'L0_attn_b_bo': _L0_attn_b_in['bo'], 'L0_ffn_w_up': _L0_ffn_in['w_up'], 'L0_ffn_w_down': _L0_ffn_in['w_down']}
    _x0 = _d['L0_attn_a_x']
    _d['L0_attn_a_x'] = jax.random.normal(jax.random.fold_in(jax.random.key(seed), 1), (8, 512, 128), dtype=_x0.dtype)
    del _x0
    return _d

def reference(L0_attn_a_x, L0_attn_a_gamma, L0_attn_a_beta, L0_attn_a_W_in, L0_attn_a_W_conv, L0_attn_a_b_conv, L0_attn_a_W_x, L0_attn_a_W_dt, L0_attn_a_b_dt, L0_attn_a_A_log, L0_attn_a_Dskip, L0_attn_a_W_out, L0_attn_b_W1, L0_attn_b_b1, L0_attn_b_W2, L0_attn_b_b2, L0_attn_b_Wz, L0_attn_b_bz, L0_attn_b_Wh, L0_attn_b_bh, L0_attn_b_Wo, L0_attn_b_bo, L0_ffn_w_up, L0_ffn_w_down):

    def _L0_attn_a_ref(x, gamma, beta, W_in, W_conv, b_conv, W_x, W_dt, b_dt, A_log, Dskip, W_out):
        import jax, jax.numpy as jnp
        import numpy as np
        from jax import lax
        D_MODEL = 128
        EXPAND = 2
        D_INNER = EXPAND * D_MODEL
        D_STATE = 16
        D_CONV = 4
        DT_RANK = (D_MODEL + 15) // 16
        BATCH, SEQ = (2, 128)

        def _layernorm(x, gamma, beta, eps=1e-05):
            mu = jnp.mean(x, axis=-1, keepdims=True)
            var = jnp.mean(jnp.square(x - mu), axis=-1, keepdims=True)
            return (x - mu) * lax.rsqrt(var + eps) * gamma + beta

        def _mamba_block(x, gamma, beta, W_in, W_conv, b_conv, W_x, W_dt, b_dt, A_log, Dskip, W_out):
            h = _layernorm(x, gamma, beta)
            xz = h @ W_in
            xi, z = jnp.split(xz, 2, axis=-1)
            xt = xi.transpose(0, 2, 1)
            conv = lax.conv_general_dilated(xt, W_conv[:, None, :], window_strides=(1,), padding=[(D_CONV - 1, 0)], feature_group_count=D_INNER)
            u = jax.nn.silu(conv + b_conv[None, :, None]).transpose(0, 2, 1)
            x_dbl = u @ W_x
            dt_r = x_dbl[..., :DT_RANK]
            Bm = x_dbl[..., DT_RANK:DT_RANK + D_STATE]
            Cm = x_dbl[..., DT_RANK + D_STATE:]
            dt = jax.nn.softplus(dt_r @ W_dt + b_dt)
            A = -jnp.exp(A_log)

            def step(hstate, inp):
                dt_s, B_s, C_s, u_s = inp
                dA = jnp.exp(dt_s[..., None] * A)
                hstate = dA * hstate + (dt_s * u_s)[..., None] * B_s[:, None, :]
                y = jnp.einsum('bdn,bn->bd', hstate, C_s)
                return (hstate, y)
            h0 = jnp.zeros((x.shape[0], D_INNER, D_STATE), x.dtype)
            _, ys = lax.scan(step, h0, (dt.transpose(1, 0, 2), Bm.transpose(1, 0, 2), Cm.transpose(1, 0, 2), u.transpose(1, 0, 2)))
            y = ys.transpose(1, 0, 2) + u * Dskip
            y = y * jax.nn.silu(z)
            return x + y @ W_out
        return _mamba_block(x, gamma, beta, W_in, W_conv, b_conv, W_x, W_dt, b_dt, A_log, Dskip, W_out)

    def _L0_attn_b_ref(x, W1, b1, W2, b2, Wz, bz, Wh, bh, Wo, bo):
        import jax, jax.numpy as jnp
        import numpy as np
        HID = 128
        EXP = 512

        def _min_gru(x_in, Wz, bz, Wh, bh):
            z = jax.nn.sigmoid(jnp.einsum('bse,ef->bsf', x_in, Wz) + bz)
            h_tilde = jnp.einsum('bse,ef->bsf', x_in, Wh) + bh
            a = 1.0 - z
            b = z * h_tilde

            def combine(c1, c2):
                a1, b1 = c1
                a2, b2 = c2
                return (a2 * a1, a2 * b1 + b2)
            _, h = jax.lax.associative_scan(combine, (a, b), axis=1)
            return h
        x_in = jax.nn.silu(jnp.einsum('bsd,de->bse', x, W1) + b1)
        x_skip = jax.nn.silu(jnp.einsum('bsd,de->bse', x, W2) + b2)
        h = _min_gru(x_in, Wz, bz, Wh, bh)
        return jnp.einsum('bse,ed->bsd', x_skip + h, Wo) + bo

    def _L0_ffn_ref(x, w_up, w_down):
        import jax, jax.numpy as jnp
        import numpy as np
        EPS = 1e-08

        def _ternary_linear(x, w):
            alpha = jnp.mean(jnp.abs(w))
            w_t = jnp.sign(w) * (jnp.abs(w) > 0.5 * alpha).astype(w.dtype)
            w_q = w + jax.lax.stop_gradient(w_t - w)
            d = x.shape[-1]
            rms = jnp.sqrt(jnp.sum(x * x, axis=-1, keepdims=True)) / jnp.sqrt(jnp.asarray(d, x.dtype))
            x_norm = x / (rms + EPS)
            return jnp.einsum('bsd,fd->bsf', x_norm, w_q)
        h = jax.nn.gelu(_ternary_linear(x, w_up), approximate=False)
        return _ternary_linear(h, w_down)
    x = L0_attn_a_x
    x = x + _L0_attn_a_ref(_layernorm(x, axis=-1), L0_attn_a_gamma, L0_attn_a_beta, L0_attn_a_W_in, L0_attn_a_W_conv, L0_attn_a_b_conv, L0_attn_a_W_x, L0_attn_a_W_dt, L0_attn_a_b_dt, L0_attn_a_A_log, L0_attn_a_Dskip, L0_attn_a_W_out)
    x = x + _L0_ffn_ref(_layernorm(x, axis=-1), L0_ffn_w_up, L0_ffn_w_down)
    x = x + _L0_attn_b_ref(_layernorm(x, axis=-1), L0_attn_b_W1, L0_attn_b_b1, L0_attn_b_W2, L0_attn_b_b2, L0_attn_b_Wz, L0_attn_b_bz, L0_attn_b_Wh, L0_attn_b_bh, L0_attn_b_Wo, L0_attn_b_bo)
    x = x + _L0_ffn_ref(_layernorm(x, axis=-1), L0_ffn_w_up, L0_ffn_w_down)
    return x

_drawn_inputs = setup_inputs


def setup_inputs(seed=0):
    import zlib

    import numpy as np

    out = dict(_drawn_inputs(seed))
    spreads = {'L0_attn_a_gamma': (1.0, 0.2),
     'L0_attn_a_beta': (0.0, 0.1),
     'L0_attn_a_b_conv': (0.0, 0.1),
     'L0_attn_a_Dskip': (1.0, 0.2)}
    factors = {}
    for name, (base, spread) in spreads.items():
        noise = np.random.default_rng([zlib.crc32(name.encode()), seed]).standard_normal(out[name].shape)
        drawn = base * np.exp(spread * noise) if base else spread * noise
        out[name] = jnp.asarray(drawn.astype(out[name].dtype))
    for name, factor in factors.items():
        out[name] = (out[name] * factor).astype(out[name].dtype)
    return out
```

```python
from contextlib import ExitStack

import concourse.bass as bass
from concourse import mybir

F32 = mybir.dt.float32
F32R = mybir.dt.float32r
ALU = mybir.AluOpType
ACT = mybir.ActivationFunctionType
AX_X = mybir.AxisListType.X

P = 128
ROWS, SEQ, D = 8, 512, 128
TILES = SEQ // P
INNER = 256
HALVES = INNER // P
STATE = 16
TAPS = 4
RANK = 8
FF = 512
FB = FF // P
UNITS = STATE * HALVES
LN_EPS = 1e-5
RMS_EPS = 1e-8

FFN1, GRU, FFN2 = 0, 7, 25
TAIL_PRODUCTS = 32
T_NORM, T_UP, T_DOWN, T_SUMSQ = 0, 1, 5, 6
G_NORM, G_IN, G_SKIP, G_GATE, G_OUT = 7, 8, 12, 16, 24
PER_BANK = TAIL_PRODUCTS // 2


def build(nc, x, gamma, beta, W_in, W_conv, b_conv, W_x, W_dt, b_dt, A_log, Dskip, W_out,
          W1, b1, W2, b2, Wz, bz, Wh, bh, Wo, bo, w_up, w_down, out):
    ctx = ExitStack()
    with ctx:
        def sb(name, shape, dt=F32):
            return ctx.enter_context(nc.sbuf_tensor(name, shape, dt))

        def sem(name):
            return ctx.enter_context(nc.semaphore(name))

        ident = sb("ident", [P, P])
        ones = sb("ones", [P, P])
        minus_half = sb("minus_half", [P, 8])
        plus_half = sb("plus_half", [P, 8])
        eps_pair = sb("eps_pair", [P, 2, TILES])
        pick = sb("pick", [P, 2 * STATE])
        select = sb("select", [P, 2 * STATE, P], F32R)
        gamma_c, beta_c = sb("gamma_c", [P, 1]), sb("beta_c", [P, 1])
        taps_c = sb("taps_c", [P, HALVES, TAPS])
        b_conv_c, b_dt_c = sb("b_conv_c", [P, HALVES]), sb("b_dt_c", [P, HALVES])
        skip_c = sb("skip_c", [P, HALVES])
        decay_c = sb("decay_c", [P, HALVES, STATE])
        win_hi, win_lo = sb("win_hi", [P, 2 * INNER], F32R), sb("win_lo", [P, 2 * INNER], F32R)
        wx_rep = sb("wx_rep", [P, HALVES, P])
        wdt_f = sb("wdt_f", [P, INNER])
        wdt_hi, wdt_lo = sb("wdt_hi", [P, INNER], F32R), sb("wdt_lo", [P, INNER], F32R)
        wout_sb = sb("wout_sb", [P, HALVES, D])
        w12_hi, w12_lo = sb("w12_hi", [P, 2 * FF], F32R), sb("w12_lo", [P, 2 * FF], F32R)
        wzh_hi = sb("wzh_hi", [P, FB, 2 * FF], F32R)
        wzh_lo = sb("wzh_lo", [P, FB, 2 * FF], F32R)
        wo_sb = sb("wo_sb", [P, FB, D])
        b1_c, b2_c, bz_c, bh_c = (sb(n, [P, FB]) for n in ("b1_c", "b2_c", "bz_c", "bh_c"))
        bo_tok = sb("bo_tok", [P, TILES, D])
        up_t = sb("up_t", [P, FF], F32R)
        down_t = sb("down_t", [P, FB, D])
        abs_sum = sb("abs_sum", [P, 2])
        thr, thr_neg = sb("thr", [P, 2]), sb("thr_neg", [P, 2])

        x_tok = sb("x_tok", [P, TILES, D])
        m_stat, m_mv = sb("m_stat", [P, TILES, 6]), sb("m_mv", [P, TILES, 2])
        m_vv, m_root = sb("m_vv", [P, 2, TILES]), sb("m_root", [P, 2, TILES])
        m_gain, m_shift = sb("m_gain", [P, TILES]), sb("m_shift", [P, TILES])
        h_tok = sb("h_tok", [P, TILES, D])
        base_tok = sb("base_tok", [P, TILES, D])
        h_f = h_tok[:, :, :].rearrange("p j d -> p (j d)")
        h_hi, h_lo = sb("h_hi", [P, SEQ], F32R), sb("h_lo", [P, SEQ], F32R)
        conv = sb("conv", [P, HALVES, SEQ])
        u = sb("u", [P, HALVES, SEQ])
        z_tok = sb("z_tok", [P, TILES, INNER])
        xd = sb("xd", [P, SEQ], F32R)
        sp_abs, sp_relu = conv, sb("sp_relu", [P, HALVES, SEQ])
        win_f = sp_relu[:, 0, :]
        dt = sb("dt", [P, HALVES, SEQ])
        dtu = sb("dtu", [P, HALVES, SEQ])
        skip_u = sb("skip_u", [P, HALVES, SEQ])
        b_all = sb("b_all", [P, 2, SEQ])
        inflow = sb("inflow", [P, 2, SEQ])
        state = sb("state", [P, 3, SEQ])
        read = sb("read", [P, 2, SEQ])
        gated_tok, gated = z_tok, skip_u

        x1_tok = sb("x1_tok", [P, TILES, D])
        x2_tok, x2b_tok = sb("x2_tok", [P, TILES, D]), sb("x2b_tok", [P, TILES, D])
        x3_tok = sb("x3_tok", [P, TILES, D])
        out_tok = sb("out_tok", [P, TILES, D])
        t_stat, t_mv = sb("t_stat", [P, TILES, 6]), sb("t_mv", [P, TILES, 2])
        t_vv, t_root = sb("t_vv", [P, 2, TILES]), sb("t_root", [P, 2, TILES])
        t_den, t_scale = sb("t_den", [P, TILES]), sb("t_scale", [P, TILES])
        t_ms, t_rms = sb("t_ms", [P, TILES]), sb("t_rms", [P, TILES])
        t_rden, t_rscale = sb("t_rden", [P, TILES]), sb("t_rscale", [P, TILES])
        n_tok = sb("n_tok", [P, TILES, D])
        n_hi, n_lo = sb("n_hi", [P, SEQ], F32R), sb("n_lo", [P, SEQ], F32R)
        wide = sb("wide", [P, 2 * FB, SEQ])
        act_f = wide[:, 0:FB, :]
        skip_f = wide[:, FB:2 * FB, :]
        wzh_f = wide[:, :, :].rearrange("p a s -> p (a s)").rearrange("p (k n) -> p k n", k=FB)
        in_hi, in_lo = sb("in_hi", [P, FB, SEQ], F32R), sb("in_lo", [P, FB, SEQ], F32R)
        sq = sb("sq", [P, FB, SEQ])
        mixed = sq
        w12_f = sq[:, 0:2, :].rearrange("p a s -> p (a s)")
        sq_sum = sb("sq_sum", [P, SEQ])
        gate = sb("gate", [P, 2, SEQ])
        keep = sb("keep", [P, 2, SEQ])
        new = sb("new", [P, 2, SEQ])
        hid = sb("hid", [P, 2, SEQ])
        up_raw, up_sign = x1_tok, x2_tok
        down_raw = x3_tok[:, :, :].rearrange("p a s -> p (a s)")
        down_sign = out_tok[:, :, :].rearrange("p a s -> p (a s)")
        below = n_tok

        bank = [ctx.enter_context(nc.psum_tensor(f"bank{i}", [P, SEQ], F32)) for i in range(8)]
        dA = bank[0:2]
        b_ps, c_ps = bank[2], bank[3]
        y_ps = bank[4:6]
        work = bank[6:8]

        s_w_mix, s_w_tail, s_w_zh = sem("w_mix"), sem("w_tail"), sem("w_zh")
        s_x_in, s_out = sem("x_in"), sem("out_stored")
        s_const, s_eye = sem("const"), sem("eye")
        s_passed = sem("passed")
        s_pick, s_select = sem("pick_ready"), sem("select_ready")
        s_expA, s_A = sem("exp_A"), sem("A_ready")
        s_win_hi, s_win = sem("win_hi_ready"), sem("win_ready")
        s_wdt_hi, s_wdt = sem("wdt_hi_ready"), sem("wdt_ready")
        s_wxz = sem("zeros_ready")
        s_hi12, s_lo12, s_hizh, s_lozh = sem("w12_hi"), sem("w12_lo"), sem("wzh_hi_s"), sem("wzh_lo_s")
        s_abs, s_abs_all, s_thr, s_below, s_sign = (sem("abs_sums"), sem("abs_all"), sem("thresholds"),
                                                    sem("below_mask"), sem("signs"))
        s_tern_t, s_tern = sem("ternary_transposed"), sem("ternary_ready")

        s_mstat, s_mmv, s_mvv, s_mroot = sem("m_stat_s"), sem("m_mv_s"), sem("m_vv_s"), sem("m_root_s")
        s_mgs, s_htok, s_base = sem("m_gain_shift"), sem("h_tok_ready"), sem("base_ready")
        s_ht, s_hhi, s_hlo = sem("h_transposed"), sem("h_hi_ready"), sem("h_lo_ready")
        s_xi, s_z, s_ztok = sem("xi_full"), sem("z_full"), sem("z_tok_ready")
        s_conv, s_u, s_skip = sem("conv_steps"), sem("u_ready"), sem("skip_ready")
        s_xdbl, s_xdhi, s_xdlo = sem("xdbl_full"), sem("xd_hi_ready"), sem("xd_lo_ready")
        s_dtp, s_sparg, s_spexp, s_spln = (sem("dt_full"), sem("softplus_args"), sem("softplus_exp"),
                                           sem("softplus_ln"))
        s_dt, s_dtu = sem("dt_ready"), sem("dtu_ready")
        s_bps, s_cps, s_ball = sem("b_full"), sem("c_full"), sem("b_copied")
        s_dA, s_inflow, s_scan, s_read, s_acc = (sem("decay_ready"), sem("inflow_ready"), sem("scan_done"),
                                                 sem("read_ready"), sem("acc_done"))
        s_gtok, s_gt, s_gated = sem("gated_tok_ready"), sem("gated_transposed"), sem("gated_ready")
        s_mix, s_x1 = sem("mix_full"), sem("x1_ready")

        s_full = [sem("work_full0"), sem("work_full1")]
        s_evac = [sem("work_evac0"), sem("work_evac1")]
        s_tstat, s_tmv, s_tvv, s_troot = sem("t_stat_s"), sem("t_mv_s"), sem("t_vv_s"), sem("t_root_s")
        s_tden, s_tscale, s_ntok, s_nhi = sem("t_den_s"), sem("t_scale_s"), sem("n_tok_ready"), sem("n_hi_ready")
        s_sq, s_sq2, s_sqsum = sem("squares"), sem("square_pairs"), sem("square_sum")
        s_trms, s_trden, s_trscale = sem("t_rms_s"), sem("t_rden_s"), sem("t_rscale_s")
        s_inf, s_inlo = sem("in_f_ready"), sem("in_lo_ready")
        s_keep, s_hid, s_mixed, s_x2b = sem("keep_ready"), sem("hid_ready"), sem("mixed_ready"), sem("x2b_ready")

        def full(eng, t, g):
            eng.wait_ge(s_full[g % 2], t * PER_BANK + g // 2 + 1)

        def evacuated(eng, t, g):
            eng.wait_ge(s_evac[g % 2], t * PER_BANK + g // 2 + 1)

        def bank_free(eng, t, g):
            eng.wait_ge(s_evac[g % 2], t * PER_BANK + g // 2)

        def half(h):
            return slice(h * SEQ, h * SEQ + SEQ)

        def cols(j):
            return slice(j * P, (j + 1) * P)

        block = ctx.enter_context(nc.Block())

        @block.sync
        def _(sp):
            def load_x(b):
                if not isinstance(b, int):
                    sp.wait_ge(s_htok, b)
                    sp.wait_ge(s_base, b)
                sp.dma_start(x_tok[:, :, :], x[bass.ds(b, 1), :, :].rearrange("a (j p) d -> (a p) j d", p=P)
                             ).then_inc(s_x_in, 16)

            load_x(0)
            for dst, src in ((gamma_c[:, :], gamma.rearrange("(p a) -> p a", a=1)),
                             (beta_c[:, :], beta.rearrange("(p a) -> p a", a=1)),
                             (win_f, W_in),
                             (taps_c[:, :, :], W_conv.rearrange("(h p) k -> p h k", p=P)),
                             (b_conv_c[:, :], b_conv.rearrange("(h p) -> p h", p=P)),
                             (b_dt_c[:, :], b_dt.rearrange("(h p) -> p h", p=P)),
                             (decay_c[:, :, :], A_log.rearrange("(h p) n -> p h n", p=P)),
                             (skip_c[:, :], Dskip.rearrange("(h p) -> p h", p=P)),
                             (wout_sb[:, :, :], W_out.rearrange("(h p) n -> p h n", p=P))):
                sp.dma_start(dst, src, allow_slow_non_contiguous=True).then_inc(s_w_mix, 16)
            sp.wait_ge(s_wxz, 2)
            wx = W_x.rearrange("(h p) r -> p h r", p=P)
            for at in (0, 2 * STATE):
                sp.dma_start(wx_rep[:, :, at:at + 2 * STATE], wx[:, :, RANK:RANK + 2 * STATE]).then_inc(s_w_mix, 16)
            for at in (64, 96):
                sp.dma_start(wx_rep[:, :, at:at + RANK], wx[:, :, 0:RANK]).then_inc(s_w_mix, 16)
                sp.dma_start(wdt_f[at:at + RANK, :], W_dt).then_inc(s_w_mix, 16)
            for dst, src in ((up_raw[:, :, :], w_up.rearrange("(k p) d -> p k d", p=P)),
                             (down_raw, w_down),
                             (w12_f[:, 0:FF], W1), (w12_f[:, FF:2 * FF], W2),
                             (b1_c[:, :], b1.rearrange("(k p) -> p k", p=P)),
                             (b2_c[:, :], b2.rearrange("(k p) -> p k", p=P)),
                             (bz_c[:, :], bz.rearrange("(k p) -> p k", p=P)),
                             (bh_c[:, :], bh.rearrange("(k p) -> p k", p=P)),
                             (wo_sb[:, :, :], Wo.rearrange("(k p) n -> p k n", p=P))):
                sp.dma_start(dst, src, allow_slow_non_contiguous=True).then_inc(s_w_tail, 16)
            for j in range(TILES):
                sp.dma_start(bo_tok[:, j, :], bo.partition_broadcast(P)).then_inc(s_w_tail, 16)
            sp.dma_start(wzh_f[:, :, 0:FF], Wz.rearrange("(k p) n -> p k n", p=P)).then_inc(s_w_zh, 16)
            sp.dma_start(wzh_f[:, :, FF:2 * FF], Wh.rearrange("(k p) n -> p k n", p=P)).then_inc(s_w_zh, 16)

            def store(t):
                evacuated(sp, t, FFN2 + T_DOWN)
                sp.dma_start(out[bass.ds(t, 1), :, :].rearrange("a (j p) d -> (a p) j d", p=P), out_tok[:, :, :]
                             ).then_inc(s_out, 16)

            with sp.Fori(1, ROWS) as b:
                load_x(b)
                store(b - 1)
            store(ROWS - 1)
            sp.wait_ge(s_out, 16 * ROWS)

        W_MIX, W_TAIL = 16 * (9 + 2 + 4), 16 * (9 + TILES)

        @block.gpsimd
        def _(pool):
            pool.memset(wx_rep[:, :, :], 0.0).then_inc(s_wxz, 1)
            pool.memset(wdt_f[:, :], 0.0).then_inc(s_wxz, 1)
            pool.memset(ones[:, :], 1.0).then_inc(s_const, 1)
            pool.memset(minus_half[:, :], -0.5).then_inc(s_const, 1)
            pool.memset(plus_half[:, :], 0.5).then_inc(s_const, 1)
            pool.memset(eps_pair[:, 0, :], 0.0).then_inc(s_const, 1)
            pool.memset(eps_pair[:, 1, :], LN_EPS).then_inc(s_const, 1)
            pool.memset(ident[:, :], 0.0).then_inc(s_eye, 1)
            pool.wait_ge(s_eye, 1)
            pool.affine_select(out=ident[:, :], in_=ident[:, :], compare_op=ALU.not_equal, fill=1.0,
                               base=0, pattern=[[-1, P]], channel_multiplier=1).then_inc(s_eye, 1)

            def split_weights():
                pool.wait_ge(s_hi12, 1)
                pool.tensor_tensor(w12_lo[:, :], w12_f, w12_hi[:, :].bitcast(F32), ALU.subtract
                                   ).then_inc(s_lo12, 1)
                for k in range(FB):
                    pool.wait_ge(s_hizh, k + 1)
                    pool.tensor_tensor(wzh_lo[:, k, :], wzh_f[:, k, :], wzh_hi[:, k, :].bitcast(F32), ALU.subtract
                                       ).then_inc(s_lozh, 1)

            def mix_root(b):
                pool.wait_ge(s_mvv, b + 1)
                pool.tensor_tensor(m_root[:, :, :].rearrange("p a j -> p (a j)"),
                                   m_vv[:, :, :].rearrange("p a j -> p (a j)"), minus_half[:, :], ALU.pow
                                   ).then_inc(s_mroot, 1)

            def mix_base(b):
                pool.wait_ge(s_mgs, 2 * b + 2)
                pool.wait_ge(s_x1, b)
                pool.sem_inc(s_passed)
                for j in range(TILES):
                    last = pool.tensor_scalar(base_tok[:, j, :], x_tok[:, j, :], m_gain[:, j:j + 1],
                                              m_shift[:, j:j + 1], ALU.mult, ALU.add)
                last.then_inc(s_base, 1)

            def mix_h_lo(b):
                pool.wait_ge(s_hhi, b + 1)
                pool.wait_ge(s_z, 2 * b)
                pool.tensor_tensor(h_lo[:, :], h_f, h_hi[:, :].bitcast(F32), ALU.subtract).then_inc(s_hlo, 1)

            def mix_dt(b):
                pool.wait_ge(s_spln, b + 1)
                pool.wait_ge(s_dA, UNITS * b)
                pool.tensor_tensor(dt[:, :, :], sp_relu[:, :, :], sp_abs[:, :, :], ALU.add).then_inc(s_dt, 1)
                pool.wait_ge(s_dt, b + 1)
                pool.wait_ge(s_u, 2 * b + 2)
                pool.tensor_tensor(dtu[:, :, :], dt[:, :, :], u[:, :, :], ALU.mult).then_inc(s_dtu, 1)

            def mix_inflow(b, k):
                n, h = k // HALVES, k % HALVES
                if k == 0:
                    pool.wait_ge(s_dtu, b + 1)
                pool.wait_ge(s_ball, STATE * b + n + 1)
                pool.wait_ge(s_scan, UNITS * b + max(k - 1, 0))
                pool.tensor_tensor(inflow[:, k % 2, :], dtu[:, h, :], b_all[:, n % 2, :], ALU.mult
                                   ).then_inc(s_inflow, 1)

            def norm_root(t, m):
                pool.wait_ge(s_tvv, 3 * t + m + 1)
                pool.tensor_tensor(t_root[:, :, :].rearrange("p a j -> p (a j)"),
                                   t_vv[:, :, :].rearrange("p a j -> p (a j)"),
                                   (minus_half if m == 1 else plus_half)[:, :], ALU.pow).then_inc(s_troot, 1)

            def ffn_sumsq(t, f):
                pool.wait_ge(s_sq, FB * (2 * t + f) + 4)
                pool.tensor_tensor(sq[:, 0:2, :], sq[:, 0:2, :], sq[:, 2:4, :], ALU.add).then_inc(s_sq2, 1)
                pool.wait_ge(s_sq2, 2 * t + f + 1)
                pool.tensor_tensor(sq_sum[:, :], sq[:, 0, :], sq[:, 1, :], ALU.add).then_inc(s_sqsum, 1)

            def ffn_rms(t, f, base):
                evacuated(pool, t, base + T_SUMSQ)
                pool.tensor_tensor(t_rms[:, :], t_ms[:, :], plus_half[:, 0:TILES], ALU.pow).then_inc(s_trms, 1)

            def gru_in_lo(t, j):
                evacuated(pool, t, G_IN + j)
                pool.tensor_tensor(in_lo[:, j, :], act_f[:, j, :], in_hi[:, j, :].bitcast(F32), ALU.subtract
                                   ).then_inc(s_inlo, 1)

            def gru_keep(t, j):
                evacuated(pool, t, G_GATE + 2 * j)
                pool.wait_ge(s_hid, FB * t + max(j - 1, 0))
                pool.sem_inc(s_passed)
                pool.tensor_scalar(keep[:, j % 2, :], gate[:, j % 2, :], -1.0, 1.0, ALU.mult, ALU.add
                                   ).then_inc(s_keep, 1)

            def gru_mixed(t, j):
                pool.wait_ge(s_hid, FB * t + j + 1)
                pool.tensor_tensor(mixed[:, j, :], hid[:, j % 2, :], skip_f[:, j, :], ALU.add).then_inc(s_mixed, 1)

            def gru_x2b(t):
                evacuated(pool, t, FFN1 + T_DOWN)
                pool.tensor_tensor(x2b_tok[:, :, :], x2_tok[:, :, :], bo_tok[:, :, :], ALU.add).then_inc(s_x2b, 1)

            def mix(b):
                mix_root(b)
                mix_base(b)
                mix_h_lo(b)
                mix_dt(b)
                for k in range(UNITS):
                    mix_inflow(b, k)

            def ffn(t, f, base):
                norm_root(t, 2 * f)
                ffn_sumsq(t, f)
                ffn_rms(t, f, base)

            def tail(t):
                ffn(t, 0, FFN1)
                norm_root(t, 1)
                gru_x2b(t)
                for j in range(FB):
                    gru_in_lo(t, j)
                for j in range(FB):
                    gru_keep(t, j)
                    gru_mixed(t, j)
                ffn(t, 1, FFN2)

            pool.wait_ge(s_const, 5)
            pool.wait_ge(s_w_tail, W_TAIL)
            split_weights()
            with pool.Fori(0, ROWS) as b:
                mix(b)
                tail(b)

        @block.scalar
        def _(act):
            def prepare():
                act.wait_ge(s_w_mix, W_MIX)
                act.activation(decay_c[:, :, :], decay_c[:, :, :], ACT.Exp).then_inc(s_expA, 1)
                act.wait_ge(s_w_tail, W_TAIL)
                act.activation(w12_hi[:, :], w12_f, ACT.Copy).then_inc(s_hi12, 1)
                act.wait_ge(s_w_zh, 32)
                for k in range(FB):
                    act.activation(wzh_hi[:, k, :], wzh_f[:, k, :], ACT.Copy).then_inc(s_hizh, 1)
                act.wait_ge(s_tern_t, 1)
                act.activation(up_t[:, :], work[0][:, :], ACT.Copy).then_inc(s_tern, 1)
                act.wait_ge(s_tern_t, 2)
                act.activation(down_t[:, :, :].rearrange("p k d -> p (k d)"), work[1][:, :], ACT.Copy
                               ).then_inc(s_tern, 1)

            def mix_h(b):
                act.wait_ge(s_ht, b + 1)
                act.wait_ge(s_hlo, b)
                act.activation(h_f, b_ps[:, :], ACT.Identity, bias=beta_c[:, 0:1], scale=gamma_c[:, 0:1])
                act.activation(h_hi[:, :], b_ps[:, :], ACT.Identity, bias=beta_c[:, 0:1], scale=gamma_c[:, 0:1]
                               ).then_inc(s_hhi, 1)

            def mix_z(b, i):
                act.wait_ge(s_z, 2 * b + i + 1)
                act.activation(z_tok[:, 2 * i:2 * i + 2, :].rearrange("p j c -> p (j c)"), y_ps[i][:, :], ACT.Silu
                               ).then_inc(s_ztok, 1)

            def mix_u(b, h):
                act.wait_ge(s_conv, HALVES * TAPS * b + HALVES * (TAPS - 1) + h + 1)
                act.wait_ge(s_dtu, b)
                act.activation(u[:, h, :], conv[:, h, :], ACT.Silu).then_inc(s_u, 1)

            def mix_xd(b):
                act.wait_ge(s_xdbl, b + 1)
                act.activation(xd[:, :], b_ps[:, :], ACT.Copy).then_inc(s_xdhi, 1)

            def mix_softplus(b):
                act.wait_ge(s_dt, b)
                for h in range(HALVES):
                    act.wait_ge(s_dtp, HALVES * b + h + 1)
                    act.activation(sp_relu[:, h, :], dA[h][:, :], ACT.Relu, bias=b_dt_c[:, h:h + 1])
                    act.activation(sp_abs[:, h, :], dA[h][:, :], ACT.Abs, bias=b_dt_c[:, h:h + 1]
                                   ).then_inc(s_sparg, 1)
                act.wait_ge(s_sparg, HALVES * b + HALVES)
                act.activation(sp_abs[:, :, :], sp_abs[:, :, :], ACT.Exp, scale=-1.0).then_inc(s_spexp, 1)
                act.wait_ge(s_spexp, b + 1)
                act.activation(sp_abs[:, :, :], sp_abs[:, :, :], ACT.Ln, bias=1.0).then_inc(s_spln, 1)

            def mix_b(b, n):
                act.wait_ge(s_bps, STATE * b + n + 1)
                act.wait_ge(s_inflow, UNITS * b + max(2 * (n - 1), 0))
                act.activation(b_all[:, n % 2, :], b_ps[:, :], ACT.Copy).then_inc(s_ball, 1)

            def mix_decay(b, k):
                n, h = k // HALVES, k % HALVES
                if k == 0:
                    act.wait_ge(s_dt, b + 1)
                act.wait_ge(s_scan, UNITS * b + max(k - 1, 0))
                act.activation(dA[k % 2][:, :], dt[:, h, :], ACT.Exp, scale=decay_c[:, h, n:n + 1]
                               ).then_inc(s_dA, 1)

            def mix_gated(b, h):
                act.wait_ge(s_gt, HALVES * b + h + 1)
                act.activation(gated[:, h, :], dA[h][:, :], ACT.Copy).then_inc(s_gated, 1)

            def norm_hi(t, m, g):
                full(act, t, g)
                act.activation(n_hi[:, :], work[g % 2][:, :], ACT.Copy).then_inc(s_nhi, 1)

            def ffn_gelu(t, f, base, j):
                g = base + T_UP + j
                full(act, t, g)
                act.activation(act_f[:, j, :], work[g % 2][:, :], ACT.Gelu).then_inc(s_evac[g % 2], 1)

            def ffn_square(t, f, base, j):
                evacuated(act, t, base + T_UP + j)
                act.activation(sq[:, j, :], act_f[:, j, :], ACT.Square).then_inc(s_sq, 1)

            def gru_in(t, j):
                g = G_IN + j
                full(act, t, g)
                act.activation(act_f[:, j, :], work[g % 2][:, :], ACT.Silu, bias=b1_c[:, j:j + 1])
                act.activation(in_hi[:, j, :], work[g % 2][:, :], ACT.Silu, bias=b1_c[:, j:j + 1]
                               ).then_inc(s_evac[g % 2], 1)

            def gru_skip(t, j):
                g = G_SKIP + j
                full(act, t, g)
                act.activation(skip_f[:, j, :], work[g % 2][:, :], ACT.Silu, bias=b2_c[:, j:j + 1]
                               ).then_inc(s_evac[g % 2], 1)

            def gru_gate(t, j):
                g = G_GATE + 2 * j
                full(act, t, g)
                if j >= 2:
                    act.wait_ge(s_keep, FB * t + j - 1)
                    evacuated(act, t, g - 3)
                act.activation(gate[:, j % 2, :], work[g % 2][:, :], ACT.Sigmoid, bias=bz_c[:, j:j + 1]
                               ).then_inc(s_evac[g % 2], 1)

            def mix(b):
                mix_h(b)
                mix_z(b, 0)
                mix_z(b, 1)
                mix_u(b, 0)
                mix_u(b, 1)
                mix_xd(b)
                mix_softplus(b)
                for k in range(UNITS):
                    if k % HALVES == 0:
                        mix_b(b, k // HALVES)
                    mix_decay(b, k)
                mix_gated(b, 0)
                mix_gated(b, 1)

            def ffn(t, f, base):
                norm_hi(t, 2 * f, base)
                for j in range(FB):
                    ffn_gelu(t, f, base, j)
                for j in range(FB):
                    ffn_square(t, f, base, j)

            def tail(t):
                ffn(t, 0, FFN1)
                norm_hi(t, 1, G_NORM)
                for j in range(FB):
                    gru_in(t, j)
                for j in range(FB):
                    gru_skip(t, j)
                for j in range(FB):
                    gru_gate(t, j)
                ffn(t, 1, FFN2)

            prepare()
            with act.Fori(0, ROWS) as b:
                mix(b)
                tail(b)

        @block.vector
        def _(dve):
            def prepare():
                dve.wait_ge(s_eye, 2)
                dve.tensor_tensor(pick[:, :], ident[:, 0:2 * STATE], ident[:, 2 * STATE:4 * STATE], ALU.add
                                  ).then_inc(s_pick, 1)
                dve.wait_ge(s_pick, 1)
                dve.tensor_copy(select[:, :, :], pick[:, :].unsqueeze(2).broadcast_to([P, 2 * STATE, P])
                                ).then_inc(s_select, 1)
                dve.wait_ge(s_w_mix, W_MIX)
                dve.tensor_copy(win_hi[:, :], win_f).then_inc(s_win_hi, 1)
                dve.tensor_copy(wdt_hi[:, :], wdt_f[:, :]).then_inc(s_wdt_hi, 1)
                dve.wait_ge(s_win_hi, 1)
                dve.tensor_tensor(win_lo[:, :], win_f, win_hi[:, :].bitcast(F32), ALU.subtract
                                  ).then_inc(s_win, 1)
                dve.wait_ge(s_wdt_hi, 1)
                dve.tensor_tensor(wdt_lo[:, :], wdt_f[:, :], wdt_hi[:, :].bitcast(F32), ALU.subtract
                                  ).then_inc(s_wdt, 1)
                dve.wait_ge(s_expA, 1)
                dve.tensor_scalar(decay_c[:, :, :], decay_c[:, :, :], -1.0, None, ALU.mult).then_inc(s_A, 1)
                dve.wait_ge(s_w_tail, W_TAIL)
                dve.tensor_reduce(abs_sum[:, 0:1], up_raw[:, :, :].rearrange("p k d -> p (k d)"), AX_X, ALU.add,
                                  apply_absolute_value=True).then_inc(s_abs, 1)
                dve.tensor_reduce(abs_sum[:, 1:2], down_raw, AX_X, ALU.add, apply_absolute_value=True
                                  ).then_inc(s_abs, 1)
                dve.wait_ge(s_abs_all, 1)
                dve.tensor_scalar(thr[:, :], work[0][:, 0:2], 0.5 / (FF * D), None, ALU.mult).then_inc(s_thr, 1)
                dve.tensor_scalar(thr_neg[:, :], work[0][:, 0:2], -0.5 / (FF * D), None, ALU.mult
                                  ).then_inc(s_thr, 1)
                dve.wait_ge(s_thr, 2)
                for i, (raw, sign) in enumerate(((up_raw[:, :, :].rearrange("p k d -> p (k d)"),
                                                  up_sign[:, :, :].rearrange("p k d -> p (k d)")),
                                                 (down_raw, down_sign))):
                    mask = below[:, :, :].rearrange("p k d -> p (k d)")
                    dve.tensor_scalar(mask, raw, thr_neg[:, i:i + 1], None, ALU.is_lt).then_inc(s_below, 1)
                    dve.wait_ge(s_below, i + 1)
                    dve.scalar_tensor_tensor(sign, raw, thr[:, i:i + 1], mask, ALU.is_gt, ALU.subtract
                                             ).then_inc(s_sign, 1)
                    dve.wait_ge(s_sign, i + 1)

            def mix_norm(b):
                dve.wait_ge(s_x_in, 16 * b + 16)
                for j in range(TILES):
                    last = dve.bn_stats(m_stat[:, j, :], x_tok[:, j, :])
                last.then_inc(s_mstat, 1)
                dve.wait_ge(s_mstat, b + 1)
                dve.sem_inc(s_passed)
                for j in range(TILES):
                    last = dve.bn_aggr(m_mv[:, j, :], m_stat[:, j, :])
                last.then_inc(s_mmv, 1)
                dve.wait_ge(s_mmv, b + 1)
                dve.tensor_scalar(m_vv[:, 0, :], m_mv[:, :, 1], LN_EPS, None, ALU.add)
                dve.tensor_scalar(m_vv[:, 1, :], m_mv[:, :, 1], 1.0 + LN_EPS, LN_EPS * LN_EPS, ALU.mult, ALU.add
                                  ).then_inc(s_mvv, 1)

            def mix_apply(b):
                dve.wait_ge(s_mroot, b + 1)
                dve.wait_ge(s_base, b)
                dve.tensor_scalar(m_gain[:, :], m_root[:, 0, :], 1.0, None, ALU.add).then_inc(s_mgs, 1)
                dve.scalar_tensor_tensor(m_shift[:, :], m_mv[:, :, 0], -1.0, m_root[:, 0, :], ALU.mult, ALU.mult
                                         ).then_inc(s_mgs, 1)
                dve.wait_ge(s_ht, b)
                for j in range(TILES):
                    last = dve.tensor_scalar(h_tok[:, j, :], x_tok[:, j, :], m_mv[:, j, 0:1], m_root[:, 1, j:j + 1],
                                             ALU.subtract, ALU.mult)
                last.then_inc(s_htok, 1)

            def mix_conv(b):
                dve.wait_ge(s_u, HALVES * b)
                for s in range(TAPS):
                    for h in range(HALVES):
                        w = taps_c[:, h, TAPS - 1 - s:TAPS - s]
                        if s == 0:
                            dve.wait_ge(s_xi, HALVES * b + h + 1)
                            dve.tensor_scalar(conv[:, h, :], dA[h][:, :], w, b_conv_c[:, h:h + 1], ALU.mult, ALU.add
                                              ).then_inc(s_conv, 1)
                        else:
                            dve.wait_ge(s_conv, HALVES * TAPS * b + HALVES * (s - 1) + h + 1)
                            dve.scalar_tensor_tensor(conv[:, h, s:SEQ], dA[h][:, 0:SEQ - s], w, conv[:, h, s:SEQ],
                                                     ALU.mult, ALU.add).then_inc(s_conv, 1)

            def mix_xd_lo(b):
                dve.wait_ge(s_xdhi, b + 1)
                for q in (32, 96):
                    last = dve.tensor_tensor(xd[q:q + 32, :], b_ps[q:q + 32, :], xd[q:q + 32, :].bitcast(F32),
                                             ALU.subtract)
                last.then_inc(s_xdlo, 1)

            def mix_skip(b):
                dve.wait_ge(s_u, HALVES * b + HALVES)
                for h in range(HALVES):
                    last = dve.tensor_scalar(skip_u[:, h, :], u[:, h, :], skip_c[:, h:h + 1], None, ALU.mult)
                last.then_inc(s_skip, 1)

            def mix_scan(b, k):
                dve.wait_ge(s_dA, UNITS * b + k + 1)
                dve.wait_ge(s_inflow, UNITS * b + k + 1)
                dve.wait_ge(s_read, UNITS * b + max(k - 2, 0))
                dve.tensor_tensor_scan(state[:, k % 3, :], dA[k % 2][:, :], inflow[:, k % 2, :], 0.0,
                                       ALU.mult, ALU.add).then_inc(s_scan, 1)

            def mix_read(b, k):
                dve.wait_ge(s_scan, UNITS * b + k + 1)
                if k % HALVES == 0:
                    dve.wait_ge(s_cps, STATE * b + k // HALVES + 1)
                dve.wait_ge(s_acc, UNITS * b + max(k - 1, 0))
                dve.tensor_tensor(read[:, k % 2, :], state[:, k % 3, :], c_ps[:, :], ALU.mult).then_inc(s_read, 1)

            def mix_gate(b):
                dve.wait_ge(s_acc, UNITS * b + UNITS)
                dve.wait_ge(s_ztok, 2 * b + 2)
                for i in range(2):
                    dve.tensor_tensor(gated_tok[:, 2 * i:2 * i + 2, :].rearrange("p j c -> p (j c)"), y_ps[i][:, :],
                                      z_tok[:, 2 * i:2 * i + 2, :].rearrange("p j c -> p (j c)"), ALU.mult
                                      ).then_inc(s_gtok, 1)

            def mix_x1(b):
                dve.wait_ge(s_mix, b + 1)
                dve.wait_ge(s_base, b + 1)
                dve.tensor_tensor(x1_tok[:, :, :].rearrange("p j d -> p (j d)"), b_ps[:, :],
                                  base_tok[:, :, :].rearrange("p j d -> p (j d)"), ALU.add).then_inc(s_x1, 1)

            def norm_stats(t, m, src):
                for j in range(TILES):
                    last = dve.bn_stats(t_stat[:, j, :], src[:, j, :])
                last.then_inc(s_tstat, 1)
                dve.wait_ge(s_tstat, 3 * t + m + 1)
                dve.sem_inc(s_passed)
                for j in range(TILES):
                    last = dve.bn_aggr(t_mv[:, j, :], t_stat[:, j, :])
                last.then_inc(s_tmv, 1)
                dve.wait_ge(s_tmv, 3 * t + m + 1)
                for i, eps in enumerate((LN_EPS, LN_EPS) if m == 1 else (0.0, LN_EPS)):
                    last = dve.tensor_scalar(t_vv[:, i, :], t_mv[:, :, 1], eps, None, ALU.add)
                last.then_inc(s_tvv, 1)

            def norm_apply(t, m, src):
                dve.wait_ge(s_troot, 3 * t + m + 1)
                scale = t_root[:, 0, :]
                if m != 1:
                    dve.scalar_tensor_tensor(t_den[:, :], t_root[:, 1, :], RMS_EPS, t_root[:, 0, :],
                                             ALU.mult, ALU.add).then_inc(s_tden, 1)
                    dve.wait_ge(s_tden, 2 * t + m // 2 + 1)
                    dve.reciprocal(t_scale[:, :], t_den[:, :]).then_inc(s_tscale, 1)
                    dve.wait_ge(s_tscale, 2 * t + m // 2 + 1)
                    scale = t_scale
                for j in range(TILES):
                    last = dve.tensor_scalar(n_tok[:, j, :], src[:, j, :], t_mv[:, j, 0:1], scale[:, j:j + 1],
                                             ALU.subtract, ALU.mult)
                last.then_inc(s_ntok, 1)

            def norm_lo(t, m, g):
                dve.wait_ge(s_nhi, 3 * t + m + 1)
                dve.tensor_tensor(n_lo[:, :], work[g % 2][:, :], n_hi[:, :].bitcast(F32), ALU.subtract
                                  ).then_inc(s_evac[g % 2], 1)

            def ffn_ms(t, f, base):
                g = base + T_SUMSQ
                full(dve, t, g)
                dve.tensor_scalar(t_ms[:, :], work[g % 2][:, 0:TILES], 1.0 / FF, None, ALU.mult
                                  ).then_inc(s_evac[g % 2], 1)

            def ffn_out(t, f, base, src, dst):
                g = base + T_DOWN
                dve.wait_ge(s_trms, 2 * t + f + 1)
                dve.tensor_scalar(t_rden[:, :], t_rms[:, :], RMS_EPS, None, ALU.add).then_inc(s_trden, 1)
                dve.wait_ge(s_trden, 2 * t + f + 1)
                dve.reciprocal(t_rscale[:, :], t_rden[:, :]).then_inc(s_trscale, 1)
                dve.wait_ge(s_trscale, 2 * t + f + 1)
                full(dve, t, g)
                if f == 1:
                    dve.wait_ge(s_out, 16 * t)
                for j in range(TILES):
                    last = dve.scalar_tensor_tensor(dst[:, j, :], work[g % 2][:, cols(j)], t_rscale[:, j:j + 1],
                                                    src[:, j, :], ALU.mult, ALU.add)
                last.then_inc(s_evac[g % 2], 1)

            def gru_new(t, j):
                g = G_GATE + 2 * j + 1
                full(dve, t, g)
                evacuated(dve, t, g - 1)
                dve.scalar_tensor_tensor(new[:, j % 2, :], work[g % 2][:, :], bh_c[:, j:j + 1], gate[:, j % 2, :],
                                         ALU.add, ALU.mult).then_inc(s_evac[g % 2], 1)

            def gru_scan(t, j):
                evacuated(dve, t, G_GATE + 2 * j + 1)
                dve.wait_ge(s_keep, FB * t + j + 1)
                dve.wait_ge(s_mixed, FB * t + max(j - 1, 0))
                dve.tensor_tensor_scan(hid[:, j % 2, :], keep[:, j % 2, :], new[:, j % 2, :], 0.0,
                                       ALU.mult, ALU.add).then_inc(s_hid, 1)

            def gru_out(t):
                full(dve, t, G_OUT)
                dve.wait_ge(s_x2b, t + 1)
                dve.tensor_tensor(x3_tok[:, :, :].rearrange("p j d -> p (j d)"), work[G_OUT % 2][:, :],
                                  x2b_tok[:, :, :].rearrange("p j d -> p (j d)"), ALU.add
                                  ).then_inc(s_evac[G_OUT % 2], 1)

            def mix(b):
                mix_norm(b)
                mix_apply(b)
                mix_conv(b)
                mix_skip(b)
                mix_xd_lo(b)
                for k in range(UNITS + 1):
                    if k < UNITS:
                        mix_scan(b, k)
                    if k:
                        mix_read(b, k - 1)
                mix_gate(b)
                mix_x1(b)

            def tail(t):
                dve.wait_ge(s_x1, t + 1)
                norm_stats(t, 0, x1_tok)
                norm_apply(t, 0, x1_tok)
                norm_lo(t, 0, FFN1)
                ffn_ms(t, 0, FFN1)
                ffn_out(t, 0, FFN1, x1_tok, x2_tok)
                evacuated(dve, t, FFN1 + T_DOWN)
                norm_stats(t, 1, x2_tok)
                norm_apply(t, 1, x2_tok)
                norm_lo(t, 1, G_NORM)
                for j in range(FB):
                    gru_new(t, j)
                    gru_scan(t, j)
                gru_out(t)
                evacuated(dve, t, G_OUT)
                norm_stats(t, 2, x3_tok)
                norm_apply(t, 2, x3_tok)
                norm_lo(t, 2, FFN2)
                ffn_ms(t, 1, FFN2)
                ffn_out(t, 1, FFN2, x3_tok, out_tok)

            dve.wait_ge(s_const, 5)
            prepare()
            with dve.Fori(0, ROWS) as b:
                mix(b)
                tail(b)

        @block.tensor
        def _(pe):
            def three(dst, w_hi, w_lo, r_hi, r_lo, start=True, stop=True):
                pe.matmul(dst, w_hi, r_hi, start=start, stop=False)
                pe.matmul(dst, w_lo, r_hi, start=False, stop=False)
                return pe.matmul(dst, w_hi, r_lo, start=False, stop=stop)

            def prepare():
                pe.wait_ge(s_const, 5)
                pe.wait_ge(s_eye, 2)
                pe.wait_ge(s_abs, 2)
                pe.matmul(work[0][:, 0:2], ones[:, :], abs_sum[:, :], start=True, stop=True).then_inc(s_abs_all, 1)
                pe.wait_ge(s_sign, 1)
                for k in range(FB):
                    last = pe.transpose(work[0][:, cols(k)], up_sign[:, k, :], ident[:, :])
                last.then_inc(s_tern_t, 1)
                pe.wait_ge(s_sign, 2)
                for k in range(FB):
                    last = pe.transpose(work[1][:, cols(k)], down_sign[:, cols(k)], ident[:, :])
                last.then_inc(s_tern_t, 1)
                pe.wait_ge(s_win, 1)
                pe.wait_ge(s_wdt, 1)
                pe.wait_ge(s_select, 1)
                pe.wait_ge(s_A, 1)
                pe.wait_ge(s_tern, 2)
                pe.wait_ge(s_lo12, 1)
                pe.wait_ge(s_lozh, FB)

            def mix_ht(b):
                pe.wait_ge(s_htok, b + 1)
                pe.wait_ge(s_x1, b)
                for j in range(TILES):
                    last = pe.transpose(b_ps[:, cols(j)], h_tok[:, j, :], ident[:, :])
                last.then_inc(s_ht, 1)

            def mix_in(b):
                pe.wait_ge(s_hhi, b + 1)
                pe.wait_ge(s_hlo, b + 1)
                pe.wait_ge(s_gated, HALVES * b)
                for h in range(HALVES):
                    three(dA[h][:, :], win_hi[:, cols(h)], win_lo[:, cols(h)], h_hi[:, :], h_lo[:, :]
                          ).then_inc(s_xi, 1)
                for i in range(2):
                    for j in (2 * i, 2 * i + 1):
                        at = slice((j % 2) * INNER, (j % 2 + 1) * INNER)
                        last = three(y_ps[i][:, at], h_hi[:, cols(j)], h_lo[:, cols(j)],
                                     win_hi[:, INNER:2 * INNER], win_lo[:, INNER:2 * INNER])
                    last.then_inc(s_z, 1)

            def mix_xdbl(b):
                pe.wait_ge(s_u, HALVES * b + HALVES)
                for h in range(HALVES):
                    last = pe.matmul(b_ps[:, :], wx_rep[:, h, :], u[:, h, :], start=(h == 0), stop=(h == HALVES - 1))
                last.then_inc(s_xdbl, 1)

            def mix_dtp(b):
                pe.wait_ge(s_xdlo, b + 1)
                for h in range(HALVES):
                    pe.matmul(dA[h][:, :], wdt_hi[:, cols(h)], xd[:, :], start=True, stop=False)
                    pe.matmul(dA[h][:, :], wdt_lo[:, cols(h)], xd[:, :], start=False, stop=True).then_inc(s_dtp, 1)

            def y_region(j, h):
                at = (j % 2) * INNER + h * P
                return y_ps[j // 2][:, at:at + P]

            def mix_skip(b):
                pe.wait_ge(s_skip, b + 1)
                pe.wait_ge(s_ztok, 2 * b + 2)
                for j in range(TILES):
                    for h in range(HALVES):
                        pe.matmul(y_region(j, h), skip_u[:, h, cols(j)], ident[:, :], is_transpose=True,
                                  start=(j % 2 == 0 and h == 0), stop=False, skip_group_check=True)

            def mix_bc(b, n):
                pe.wait_ge(s_ball, STATE * b + n)
                pe.matmul(b_ps[:, :], select[:, n, :], xd[:, :], start=True, stop=True).then_inc(s_bps, 1)
                pe.wait_ge(s_read, UNITS * b + HALVES * n)
                pe.matmul(c_ps[:, :], select[:, STATE + n, :], xd[:, :], start=True, stop=True).then_inc(s_cps, 1)

            def mix_acc(b, k):
                h = k % HALVES
                pe.wait_ge(s_read, UNITS * b + k + 1)
                for j in range(TILES):
                    last = pe.matmul(y_region(j, h), read[:, k % 2, cols(j)], ident[:, :], is_transpose=True,
                                     start=False, stop=(k >= UNITS - HALVES), skip_group_check=True)
                last.then_inc(s_acc, 1)

            def mix_out(b):
                pe.wait_ge(s_gtok, 2 * b + 2)
                for h in range(HALVES):
                    for j in range(TILES):
                        last = pe.transpose(dA[h][:, cols(j)], gated_tok[:, j, cols(h)], ident[:, :])
                    last.then_inc(s_gt, 1)
                pe.wait_ge(s_gated, HALVES * b + HALVES)
                for j in range(TILES):
                    for h in range(HALVES):
                        last = pe.matmul(b_ps[:, cols(j)], gated[:, h, cols(j)], wout_sb[:, h, :],
                                         start=(h == 0), stop=(h == HALVES - 1))
                last.then_inc(s_mix, 1)

            def norm_t(t, m, g):
                pe.wait_ge(s_ntok, 3 * t + m + 1)
                bank_free(pe, t, g)
                for j in range(TILES):
                    last = pe.transpose(work[g % 2][:, cols(j)], n_tok[:, j, :], ident[:, :])
                last.then_inc(s_full[g % 2], 1)

            def ffn_up(t, f, base, j):
                g = base + T_UP + j
                if j == 0:
                    evacuated(pe, t, base + T_NORM)
                bank_free(pe, t, g)
                pe.matmul(work[g % 2][:, :], up_t[:, cols(j)], n_hi[:, :], start=True, stop=False)
                pe.matmul(work[g % 2][:, :], up_t[:, cols(j)], n_lo[:, :], start=False, stop=True
                          ).then_inc(s_full[g % 2], 1)

            def ffn_down(t, f, base):
                g = base + T_DOWN
                evacuated(pe, t, base + T_UP + 2)
                evacuated(pe, t, base + T_UP + 3)
                for j in range(TILES):
                    for k in range(FB):
                        last = pe.matmul(work[g % 2][:, cols(j)], act_f[:, k, cols(j)], down_t[:, k, :],
                                         start=(k == 0), stop=(k == FB - 1))
                last.then_inc(s_full[g % 2], 1)

            def ffn_sumsq(t, f, base):
                g = base + T_SUMSQ
                pe.wait_ge(s_sqsum, 2 * t + f + 1)
                bank_free(pe, t, g)
                for j in range(TILES):
                    last = pe.matmul(work[g % 2][:, j:j + 1], sq_sum[:, cols(j)], ones[:, 0:1], start=True, stop=True)
                last.then_inc(s_full[g % 2], 1)

            def gru_in(t, j):
                g = G_IN + j
                if j == 0:
                    evacuated(pe, t, G_NORM)
                bank_free(pe, t, g)
                three(work[g % 2][:, :], w12_hi[:, cols(j)], w12_lo[:, cols(j)], n_hi[:, :], n_lo[:, :]
                      ).then_inc(s_full[g % 2], 1)

            def gru_gate(t, i):
                g = G_GATE + i
                if i == 0:
                    pe.wait_ge(s_inlo, FB * t + FB)
                bank_free(pe, t, g)
                at = slice((i % 2) * FF + (i // 2) * P, (i % 2) * FF + (i // 2 + 1) * P)
                for k in range(FB):
                    last = three(work[g % 2][:, :], wzh_hi[:, k, at], wzh_lo[:, k, at], in_hi[:, k, :], in_lo[:, k, :],
                                 start=(k == 0), stop=(k == FB - 1))
                last.then_inc(s_full[g % 2], 1)

            def gru_out(t):
                g = G_OUT
                pe.wait_ge(s_mixed, FB * t + FB)
                bank_free(pe, t, g)
                for j in range(TILES):
                    for k in range(FB):
                        last = pe.matmul(work[g % 2][:, cols(j)], mixed[:, k, cols(j)], wo_sb[:, k, :],
                                         start=(k == 0), stop=(k == FB - 1))
                last.then_inc(s_full[g % 2], 1)

            def mix(b):
                mix_ht(b)
                mix_in(b)
                mix_xdbl(b)
                mix_dtp(b)
                mix_skip(b)
                for k in range(UNITS + 1):
                    if k < UNITS and k % HALVES == 0:
                        mix_bc(b, k // HALVES)
                    if k:
                        mix_acc(b, k - 1)
                mix_out(b)

            def ffn(t, f, base):
                norm_t(t, 2 * f, base)
                for j in range(FB):
                    ffn_up(t, f, base, j)
                ffn_down(t, f, base)
                ffn_sumsq(t, f, base)

            def tail(t):
                ffn(t, 0, FFN1)
                norm_t(t, 1, G_NORM)
                for j in range(2 * FB):
                    gru_in(t, j)
                for i in range(2 * FB):
                    gru_gate(t, i)
                gru_out(t)
                ffn(t, 1, FFN2)

            prepare()
            with pe.Fori(0, ROWS) as b:
                mix(b)
                tail(b)


_INS = ["x", "gamma", "beta", "W_in", "W_conv", "b_conv", "W_x", "W_dt", "b_dt", "A_log", "Dskip", "W_out",
        "W1", "b1", "W2", "b2", "Wz", "bz", "Wh", "bh", "Wo", "bo", "w_up", "w_down"]


def kernel(**inputs):
    import numpy as np
    import concourse.bacc as bacc
    from concourse import mybir
    from concourse.bass_utils import run_bass_kernel_spmd

    nc = bacc.Bacc("TRN2", target_bir_lowering=False, num_devices=1)
    short = {}
    for name, a in inputs.items():
        for prefix in ("L0_attn_a_", "L0_attn_b_", "L0_ffn_"):
            if name.startswith(prefix):
                short[name[len(prefix):]] = np.ascontiguousarray(a)
    arrays, args = {}, []
    for name in _INS:
        a = short[name]
        arrays[f"in_{name}"] = a
        args.append(nc.dram_tensor(f"in_{name}", a.shape, mybir.dt.from_np(a.dtype), kind="ExternalInput").ap())
    x = short["x"]
    args.append(nc.dram_tensor("out_x", x.shape, mybir.dt.from_np(x.dtype), kind="ExternalOutput").ap())
    build(nc, *args)
    r = run_bass_kernel_spmd(nc, [arrays], core_ids=[0])
    return r.results[0]["out_x"]
```

```python
from contextlib import ExitStack

import concourse.bass as bass
from concourse import mybir

F32 = mybir.dt.float32
F32R = mybir.dt.float32r
ALU = mybir.AluOpType
ACT = mybir.ActivationFunctionType
AX_X = mybir.AxisListType.X

P = 128
ROWS, SEQ, D = 8, 512, 128
TILES = SEQ // P
INNER = 256
HALVES = INNER // P
STATE = 16
TAPS = 4
RANK = 8
FF = 512
FB = FF // P
LN_EPS = 1e-5
RMS_EPS = 1e-8

GATE_EVAC = (5, 7, 13, 15)
NEW_EVAC = (6, 10, 14, 17)
SCAN = 6
BACK = SCAN + STATE
SLOTS = BACK + 2
LAG = {"a": 1, "b": 2, "c": 3}
FIRST_FULL = 3
ROUNDS = ROWS + 3

BANKS = (["b.in0", "b.in2", "b.in4", "b.in6", "a.norm1", "a.up1", "a.up3", "c.up1", "c.up3", "a.sumsq",
          "c.sumsq", "b.h0", "a.down", "c.down", "b.h2", "a.norm2", "b.out"],
         ["b.in1", "b.in3", "b.in5", "b.in7", "a.up0", "a.up2", "c.up0", "c.up2", "b.z0", "b.z1", "b.h1",
          "b.z2", "b.z3", "b.h3", "b.norm3"])
WORK_BANK = {p: k for k in range(2) for p in BANKS[k]}


def mark(i, product):
    def there(r):
        return [p for p in BANKS[WORK_BANK[product]] if LAG[p[0]] <= r < LAG[p[0]] + ROWS]
    if isinstance(i, int):
        return sum(len(there(r)) for r in range(i)) + there(i).index(product) + 1
    every = there(FIRST_FULL)
    before = sum(len(there(r)) for r in range(FIRST_FULL))
    return (i - FIRST_FULL) * len(every) + before + every.index(product) + 1


def build(nc, x, gamma, beta, W_in, W_conv, b_conv, W_x, W_dt, b_dt, A_log, Dskip, W_out,
          W1, b1, W2, b2, Wz, bz, Wh, bh, Wo, bo, w_up, w_down, out):
    ctx = ExitStack()
    with ctx:
        def sb(name, shape, dt=F32):
            return ctx.enter_context(nc.sbuf_tensor(name, shape, dt))

        def sem(name):
            return ctx.enter_context(nc.semaphore(name))

        def flat(a):
            return a.rearrange("p a b -> p (a b)")

        ident = sb("ident", [P, P])
        ones = sb("ones", [P, P])
        minus_half = sb("minus_half", [P, 8])
        plus_half = sb("plus_half", [P, 8])
        pick = sb("pick", [P, 2 * STATE], F32R)
        gamma_c, beta_c = sb("gamma_c", [P, 1]), sb("beta_c", [P, 1])
        taps_c = sb("taps_c", [P, HALVES, TAPS])
        b_conv_c, b_dt_c = sb("b_conv_c", [P, HALVES]), sb("b_dt_c", [P, HALVES])
        skip_c = sb("skip_c", [P, HALVES])
        decay_c = sb("decay_c", [P, HALVES, STATE])
        win_hi, win_lo = sb("win_hi", [P, 2 * INNER], F32R), sb("win_lo", [P, 2 * INNER], F32R)
        wx_rep = sb("wx_rep", [P, HALVES, P])
        wdt_f = sb("wdt_f", [P, INNER])
        wdt_hi, wdt_lo = sb("wdt_hi", [P, INNER], F32R), sb("wdt_lo", [P, INNER], F32R)
        wout_sb = sb("wout_sb", [P, HALVES, D])
        w12_hi, w12_lo = sb("w12_hi", [P, 2 * FF], F32R), sb("w12_lo", [P, 2 * FF], F32R)
        wzh_hi = sb("wzh_hi", [P, FB, 2 * FF], F32R)
        wzh_lo = sb("wzh_lo", [P, FB, 2 * FF], F32R)
        wo_sb = sb("wo_sb", [P, FB, D])
        b1_c, b2_c, bz_c, bh_c = (sb(n, [P, FB]) for n in ("b1_c", "b2_c", "bz_c", "bh_c"))
        bzh_c = sb("bzh_c", [P, FB])
        bo_tok = sb("bo_tok", [P, TILES, D])
        up_t = sb("up_t", [P, FF], F32R)
        down_t = sb("down_t", [P, FB, D])
        abs_sum = sb("abs_sum", [P, 2])
        thr, thr_neg = sb("thr", [P, 2]), sb("thr_neg", [P, 2])

        x_tok = sb("x_tok", [P, TILES, D])
        m_stat, m_mv = sb("m_stat", [P, TILES, 6]), sb("m_mv", [P, TILES, 2])
        m_vv, m_root = sb("m_vv", [P, 2, TILES]), sb("m_root", [P, 2, TILES])
        m_gain, m_shift = sb("m_gain", [P, TILES]), sb("m_shift", [P, TILES])
        h_tok = sb("h_tok", [P, TILES, D])
        h_f = flat(h_tok[:, :, :])
        base_tok = sb("base_tok", [P, TILES, D])
        h_hi, h_lo = sb("h_hi", [P, SEQ], F32R), sb("h_lo", [P, SEQ], F32R)
        u = sb("u", [P, HALVES, SEQ])
        z_tok = sb("z_tok", [P, TILES, INNER])
        xd = sb("xd", [P, SEQ], F32R)
        dt = sb("dt", [P, HALVES, SEQ])
        dtu = sb("dtu", [P, HALVES, SEQ])
        b_all = sb("b_all", [P, 2, SEQ])
        inflow = sb("inflow", [P, 2, HALVES, SEQ])
        state = sb("state", [P, 3, HALVES, SEQ])
        sp_relu = dtu
        conv = sp_abs = state[:, 2, :, :]
        skip_u = inflow[:, 1, :, :]
        gated = inflow[:, 0, :, :]
        gated_tok = z_tok

        x1_tok, x2_tok, x2b_tok = (sb(n, [P, TILES, D]) for n in ("x1_tok", "x2_tok", "x2b_tok"))
        x3_tok = sb("x3_tok", [P, TILES, D])
        out_tok = x3_tok
        NORMS = (1, 2, 3)
        stat = {m: sb("stat%d" % m, [P, TILES, 6]) for m in NORMS}
        mv = {m: sb("mv%d" % m, [P, TILES, 2]) for m in NORMS}
        vv = {m: sb("vv%d" % m, [P, 2, TILES]) for m in NORMS}
        root = {m: sb("root%d" % m, [P, 2, TILES]) for m in NORMS}
        den = {m: sb("den%d" % m, [P, TILES]) for m in NORMS}
        scale = {m: sb("scale%d" % m, [P, TILES]) for m in NORMS}
        n_tok = {m: sb("n_tok%d" % m, [P, TILES, D]) for m in NORMS}
        n_hi = {m: sb("n_hi%d" % m, [P, SEQ], F32R) for m in NORMS}
        n_lo = {m: sb("n_lo%d" % m, [P, SEQ], F32R) for m in NORMS}
        wide = sb("wide", [P, 2 * FB, SEQ])
        act_b = sb("act_b", [P, FB, SEQ])
        mixed = sb("mixed", [P, FB, SEQ])
        gelu = {"a": wide[:, 0:FB, :], "c": act_b}
        square = {"a": wide[:, FB:2 * FB, :], "c": mixed}
        sq_sum = {"a": wide[:, FB, :], "c": mixed[:, 0, :]}
        ms = {c: sb("ms_" + c, [P, TILES]) for c in "ac"}
        rms = {c: sb("rms_" + c, [P, TILES]) for c in "ac"}
        rden = {c: sb("rden_" + c, [P, TILES]) for c in "ac"}
        rscale = {c: sb("rscale_" + c, [P, TILES]) for c in "ac"}
        in_f = act_b
        in_hi, in_lo = sb("in_hi", [P, FB, SEQ], F32R), sb("in_lo", [P, FB, SEQ], F32R)
        skip_f = sb("skip_f", [P, FB, SEQ])
        gate = sb("gate", [P, 2, SEQ])
        keep = sb("keep", [P, 2, SEQ])
        hid = sb("hid", [P, 2, SEQ])
        win_f = dtu[:, 0, :]
        w12_f = flat(skip_f[:, 0:2, :])
        wzh_f = flat(wide[:, :, :]).rearrange("p (k n) -> p k n", k=FB)
        up_raw, up_sign = x2_tok, x2b_tok
        down_raw, down_sign = flat(x3_tok[:, :, :]), flat(n_tok[2][:, :, :])
        below = flat(n_tok[3][:, :, :])

        def pb(name, shape):
            return ctx.enter_context(nc.psum_tensor(name, shape, F32))

        dA = pb("dA", [P, HALVES, SEQ])
        b_ps, c_ps = pb("b_ps", [P, SEQ]), pb("c_ps", [P, SEQ])
        y_ps = [pb("y_ps0", [P, SEQ]), pb("y_ps1", [P, SEQ])]
        work = [pb("work0", [P, SEQ]), pb("work1", [P, SEQ])]

        s_w_mix, s_w_tail, s_w_zh = sem("w_mix"), sem("w_tail"), sem("w_zh")
        s_x_in, s_out = sem("x_in"), sem("out_stored")
        s_const, s_eye = sem("const"), sem("eye")
        s_passed = sem("passed")
        s_pick = sem("pick_ready")
        s_expA, s_A = sem("exp_A"), sem("A_ready")
        s_win_hi, s_win = sem("win_hi_ready"), sem("win_ready")
        s_wdt_hi, s_wdt = sem("wdt_hi_ready"), sem("wdt_ready")
        s_wxz = sem("zeros_ready")
        s_hi12, s_lo12, s_hizh, s_lozh = sem("hi12"), sem("lo12"), sem("hizh"), sem("lozh")
        s_bzh = sem("bzh_ready")
        s_abs, s_abs_all, s_thr, s_below, s_sign = (sem("abs_sums"), sem("abs_all"), sem("thresholds"),
                                                    sem("below_mask"), sem("signs"))
        s_tern_t, s_tern = sem("ternary_transposed"), sem("ternary_ready")

        s_mstat, s_mmv, s_mvv, s_mroot = sem("m_stat_s"), sem("m_mv_s"), sem("m_vv_s"), sem("m_root_s")
        s_mgs, s_htok, s_base = sem("m_gain_shift"), sem("h_tok_ready"), sem("base_ready")
        s_ht, s_hhi, s_hlo = sem("h_transposed"), sem("h_hi_ready"), sem("h_lo_ready")
        s_xi, s_z, s_ztok = sem("xi_full"), sem("z_full"), sem("z_tok_ready")
        s_conv, s_u, s_skip, s_y0 = sem("conv_steps"), sem("u_ready"), sem("skip_ready"), sem("y_started")
        s_xdbl, s_xdhi, s_xdlo = sem("xdbl_full"), sem("xd_hi_ready"), sem("xd_lo_ready")
        s_dtp, s_sparg, s_spexp, s_spln = (sem("dt_full"), sem("softplus_args"), sem("softplus_exp"),
                                           sem("softplus_ln"))
        s_dt, s_dtu, s_zero = sem("dt_ready"), sem("dtu_ready"), sem("zero_ready")
        s_bps, s_cps, s_ball = sem("b_full"), sem("c_full"), sem("b_copied")
        s_dA, s_inflow, s_scan, s_read, s_acc = (sem("decay_ready"), sem("inflow_ready"), sem("scan_done"),
                                                 sem("read_ready"), sem("acc_done"))
        s_gtok, s_gt, s_gated = sem("gated_tok_ready"), sem("gated_transposed"), sem("gated_ready")
        s_mix, s_x1 = sem("mix_full"), sem("x1_ready")

        s_full = [sem("work_full0"), sem("work_full1")]
        s_evac = [sem("work_evac0"), sem("work_evac1")]
        s_stat, s_mv, s_vv, s_root, s_den, s_scale, s_ntok, s_nhi = (
            {m: sem("%s%d_s" % (n, m)) for m in NORMS}
            for n in ("stat", "mv", "vv", "root", "den", "scale", "n_tok", "n_hi"))
        s_sq, s_sq2, s_sqsum, s_rms, s_rden, s_rscale = (
            {c: sem("%s_%s_s" % (n, c)) for c in "ac"}
            for n in ("square", "pairs", "sum", "rms", "rden", "rscale"))
        s_inlo, s_keep, s_gate1, s_hid, s_mixed, s_x2b = (sem("in_lo_ready"), sem("keep_ready"), sem("gate1_ready"),
                                                          sem("hid_ready"), sem("mixed_ready"), sem("x2b_ready"))

        def wait(eng, s, value):
            if not (isinstance(value, int) and value == 0):
                eng.wait_ge(s, value)

        def full(eng, i, p):
            wait(eng, s_full[WORK_BANK[p]], mark(i, p))

        def evacuated(eng, i, p):
            wait(eng, s_evac[WORK_BANK[p]], mark(i, p))

        def bank_free(eng, i, p):
            wait(eng, s_evac[WORK_BANK[p]], mark(i, p) - 1)

        def work_of(p):
            return work[WORK_BANK[p]]

        def made(p):
            return s_full[WORK_BANK[p]], 1

        def emptied(p):
            return s_evac[WORK_BANK[p]], 1

        def cols(j):
            return slice(j * P, (j + 1) * P)

        def rounds(eng, mix, a, b, c, extra=None):
            def one(i, chains):
                for s in range(SLOTS):
                    if "m" in chains:
                        mix(i, s)
                    if "a" in chains:
                        a(i, i - 1, s)
                    if "c" in chains:
                        c(i, i - 3, s)
                    if "b" in chains:
                        b(i, i - 2, s)
                    if extra is not None and isinstance(i, int):
                        extra(i, s)
            one(0, "m")
            one(1, "ma")
            one(2, "mab")
            with eng.Fori(FIRST_FULL, ROWS) as i:
                one(i, "mabc")
            one(ROWS, "abc")
            one(ROWS + 1, "bc")
            one(ROWS + 2, "c")

        block = ctx.enter_context(nc.Block())

        W_MIX, W_TAIL = 16 * (9 + 2 + 4), 16 * (9 + TILES)

        @block.sync
        def _(sp):
            def load_x(b):
                wait(sp, s_htok, b)
                wait(sp, s_base, b)
                sp.dma_start(x_tok[:, :, :], x[bass.ds(b, 1), :, :].rearrange("a (j p) d -> (a p) j d", p=P)
                             ).then_inc(s_x_in, 16)

            def store(i, t):
                evacuated(sp, i, "c.down")
                sp.dma_start(out[bass.ds(t, 1), :, :].rearrange("a (j p) d -> (a p) j d", p=P), out_tok[:, :, :]
                             ).then_inc(s_out, 16)

            load_x(0)
            sp.sem_inc(s_out, 16)
            for dst, src in ((gamma_c[:, :], gamma.rearrange("(p a) -> p a", a=1)),
                             (beta_c[:, :], beta.rearrange("(p a) -> p a", a=1)),
                             (win_f, W_in),
                             (taps_c[:, :, :], W_conv.rearrange("(h p) k -> p h k", p=P)),
                             (b_conv_c[:, :], b_conv.rearrange("(h p) -> p h", p=P)),
                             (b_dt_c[:, :], b_dt.rearrange("(h p) -> p h", p=P)),
                             (decay_c[:, :, :], A_log.rearrange("(h p) n -> p h n", p=P)),
                             (skip_c[:, :], Dskip.rearrange("(h p) -> p h", p=P)),
                             (wout_sb[:, :, :], W_out.rearrange("(h p) n -> p h n", p=P))):
                sp.dma_start(dst, src, allow_slow_non_contiguous=True).then_inc(s_w_mix, 16)
            sp.wait_ge(s_wxz, 2)
            wx = W_x.rearrange("(h p) r -> p h r", p=P)
            for at in (0, 2 * STATE):
                sp.dma_start(wx_rep[:, :, at:at + 2 * STATE], wx[:, :, RANK:RANK + 2 * STATE]).then_inc(s_w_mix, 16)
            for at in (64, 96):
                sp.dma_start(wx_rep[:, :, at:at + RANK], wx[:, :, 0:RANK]).then_inc(s_w_mix, 16)
                sp.dma_start(wdt_f[at:at + RANK, :], W_dt).then_inc(s_w_mix, 16)
            for dst, src in ((up_raw[:, :, :], w_up.rearrange("(k p) d -> p k d", p=P)),
                             (down_raw, w_down),
                             (w12_f[:, 0:FF], W1), (w12_f[:, FF:2 * FF], W2),
                             (b1_c[:, :], b1.rearrange("(k p) -> p k", p=P)),
                             (b2_c[:, :], b2.rearrange("(k p) -> p k", p=P)),
                             (bz_c[:, :], bz.rearrange("(k p) -> p k", p=P)),
                             (bh_c[:, :], bh.rearrange("(k p) -> p k", p=P)),
                             (wo_sb[:, :, :], Wo.rearrange("(k p) n -> p k n", p=P))):
                sp.dma_start(dst, src, allow_slow_non_contiguous=True).then_inc(s_w_tail, 16)
            for j in range(TILES):
                sp.dma_start(bo_tok[:, j, :], bo.partition_broadcast(P)).then_inc(s_w_tail, 16)
            sp.dma_start(wzh_f[:, :, 0:FF], Wz.rearrange("(k p) n -> p k n", p=P)).then_inc(s_w_zh, 16)
            sp.dma_start(wzh_f[:, :, FF:2 * FF], Wh.rearrange("(k p) n -> p k n", p=P)).then_inc(s_w_zh, 16)

            for i in range(1, FIRST_FULL + 1):
                load_x(i)
            with sp.Fori(FIRST_FULL, ROWS - 1) as i:
                load_x(i + 1)
                store(i, i - 3)
            for i in range(ROWS - 1, ROUNDS):
                store(i, i - 3)
            sp.wait_ge(s_out, 16 * ROWS + 16)

        @block.gpsimd
        def _(pool):
            pool.memset(wx_rep[:, :, :], 0.0).then_inc(s_wxz, 1)
            pool.memset(wdt_f[:, :], 0.0).then_inc(s_wxz, 1)
            pool.memset(ones[:, :], 1.0).then_inc(s_const, 1)
            pool.memset(minus_half[:, :], -0.5).then_inc(s_const, 1)
            pool.memset(plus_half[:, :], 0.5).then_inc(s_const, 1)
            pool.memset(ident[:, :], 0.0).then_inc(s_eye, 1)
            pool.wait_ge(s_eye, 1)
            pool.affine_select(out=ident[:, :], in_=ident[:, :], compare_op=ALU.not_equal, fill=1.0,
                               base=0, pattern=[[-1, P]], channel_multiplier=1).then_inc(s_eye, 1)

            def prepare(i, s):
                if (i, s) == (0, SCAN + 2):
                    pool.wait_ge(s_hi12, 1)
                    pool.tensor_tensor(w12_lo[:, :], w12_f, w12_hi[:, :].bitcast(F32), ALU.subtract
                                       ).then_inc(s_lo12, 1)
                    pool.tensor_scalar(bzh_c[:, :], bz_c[:, :], 0.5, None, ALU.mult).then_inc(s_bzh, 1)
                if i == 0 and s in (SCAN + 4, SCAN + 6, SCAN + 8, SCAN + 10):
                    k = (s - SCAN - 4) // 2
                    pool.wait_ge(s_hizh, k + 1)
                    pool.tensor_tensor(wzh_lo[:, k, :], wzh_f[:, k, :], wzh_hi[:, k, :].bitcast(F32), ALU.subtract
                                       ).then_inc(s_lozh, 1)

            def mix_root(b):
                pool.wait_ge(s_mvv, b + 1)
                pool.tensor_tensor(flat(m_root[:, :, :]), flat(m_vv[:, :, :]), minus_half[:, :], ALU.pow
                                   ).then_inc(s_mroot, 1)

            def mix_base(b):
                pool.wait_ge(s_mgs, 2 * b + 2)
                wait(pool, s_x1, b)
                pool.sem_inc(s_passed)
                for j in range(TILES):
                    last = pool.tensor_scalar(base_tok[:, j, :], x_tok[:, j, :], m_gain[:, j:j + 1],
                                              m_shift[:, j:j + 1], ALU.mult, ALU.add)
                last.then_inc(s_base, 1)

            def mix_h_lo(b):
                pool.wait_ge(s_hhi, b + 1)
                wait(pool, s_z, 2 * b)
                pool.tensor_tensor(h_lo[:, :], h_f, h_hi[:, :].bitcast(F32), ALU.subtract).then_inc(s_hlo, 1)

            def mix_dt(b):
                pool.wait_ge(s_spln, b + 1)
                wait(pool, s_dA, STATE * b)
                pool.tensor_tensor(dt[:, :, :], sp_relu[:, :, :], sp_abs, ALU.add).then_inc(s_dt, 1)
                pool.wait_ge(s_dt, b + 1)
                pool.tensor_tensor(dtu[:, :, :], dt[:, :, :], u[:, :, :], ALU.mult).then_inc(s_dtu, 1)
                pool.wait_ge(s_dtu, b + 1)

            def mix_inflow(b, n):
                pool.wait_ge(s_ball, STATE * b + n + 1)
                if n == 0:
                    wait(pool, s_mix, b)
                if n == 1:
                    pool.wait_ge(s_y0, b + 1)
                if n >= 2:
                    pool.wait_ge(s_scan, STATE * b + n - 1)
                pool.tensor_tensor(inflow[:, n % 2, :, :], dtu[:, :, :],
                                   b_all[:, n % 2, :].unsqueeze(1).broadcast_to([P, HALVES, SEQ]), ALU.mult
                                   ).then_inc(s_inflow, 1)

            def mix(b, s):
                n = s - SCAN
                if s == 0:
                    mix_root(b)
                if s == 1:
                    mix_base(b)
                if s == 2:
                    mix_h_lo(b)
                if s == 5:
                    mix_dt(b)
                    mix_inflow(b, 0)
                if 0 <= n < STATE - 1:
                    mix_inflow(b, n + 1)

            def norm_root(t, m):
                pool.wait_ge(s_vv[m], t + 1)
                pool.tensor_tensor(flat(root[m][:, :, :]), flat(vv[m][:, :, :]),
                                   (minus_half if m == 2 else plus_half)[:, :], ALU.pow).then_inc(s_root[m], 1)

            def ffn_sumsq(t, c):
                sq = square[c]
                pool.wait_ge(s_sq[c], FB * t + 4)
                pool.tensor_tensor(sq[:, 0:2, :], sq[:, 0:2, :], sq[:, 2:4, :], ALU.add).then_inc(s_sq2[c], 1)
                pool.wait_ge(s_sq2[c], t + 1)
                pool.tensor_tensor(sq_sum[c], sq[:, 0, :], sq[:, 1, :], ALU.add).then_inc(s_sqsum[c], 1)

            def ffn_rms(i, c):
                evacuated(pool, i, c + ".sumsq")
                pool.tensor_tensor(rms[c][:, :], ms[c][:, :], plus_half[:, 0:TILES], ALU.pow).then_inc(s_rms[c], 1)

            def gru_in_lo(i, j):
                evacuated(pool, i, "b.in%d" % j)
                pool.tensor_tensor(in_lo[:, j, :], in_f[:, j, :], in_hi[:, j, :].bitcast(F32), ALU.subtract
                                   ).then_inc(s_inlo, 1)

            def gru_keep(i, t, j):
                evacuated(pool, i, "b.z%d" % j)
                if j >= 2:
                    pool.wait_ge(s_hid, FB * t + j - 1)
                pool.sem_inc(s_passed)
                pool.tensor_scalar(keep[:, j % 2, :], gate[:, j % 2, :], -0.5, 0.5, ALU.mult, ALU.add
                                   ).then_inc(s_keep, 1)
                pool.wait_ge(s_keep, FB * t + j + 1)
                pool.sem_inc(s_passed)
                pool.tensor_scalar(gate[:, j % 2, :], gate[:, j % 2, :], 1.0, 1.0, ALU.mult, ALU.add
                                   ).then_inc(s_gate1, 1)

            def x2b(i, t):
                evacuated(pool, i, "a.down")
                if not isinstance(i, int) or i >= LAG["b"]:
                    evacuated(pool, i, "b.out")
                pool.tensor_tensor(x2b_tok[:, :, :], x2_tok[:, :, :], bo_tok[:, :, :], ALU.add).then_inc(s_x2b, 1)

            def a(i, t, s):
                if s == 0:
                    norm_root(t, 1)
                if s == 4:
                    ffn_sumsq(t, "a")
                if s == 6:
                    ffn_rms(i, "a")
                if s == 10:
                    norm_root(t, 2)
                if s == 21:
                    x2b(i, t)

            def b(i, t, s):
                if s == 1:
                    for j in range(FB):
                        gru_in_lo(i, j)
                if s in GATE_EVAC:
                    gru_keep(i, t, GATE_EVAC.index(s))
                if s == 20:
                    norm_root(t, 3)

            def c(i, t, s):
                if s == 4:
                    ffn_sumsq(t, "c")
                if s == 6:
                    ffn_rms(i, "c")

            pool.wait_ge(s_const, 3)
            pool.wait_ge(s_w_tail, W_TAIL)
            rounds(pool, mix, a, b, c, prepare)

        @block.scalar
        def _(act):
            def prepare(i, s):
                if (i, s) == (0, SCAN + 1):
                    act.wait_ge(s_w_tail, W_TAIL)
                    act.activation(w12_hi[:, :], w12_f, ACT.Copy).then_inc(s_hi12, 1)
                    act.wait_ge(s_w_zh, 32)
                if i == 0 and s in (SCAN + 3, SCAN + 5, SCAN + 7, SCAN + 9):
                    k = (s - SCAN - 3) // 2
                    act.activation(wzh_hi[:, k, :], wzh_f[:, k, :], ACT.Copy).then_inc(s_hizh, 1)
                if (i, s) == (0, SCAN + 11):
                    act.wait_ge(s_tern_t, 1)
                    act.activation(up_t[:, :], work[0][:, :], ACT.Copy).then_inc(s_tern, 1)
                    act.wait_ge(s_tern_t, 2)
                    act.activation(flat(down_t[:, :, :]), work[1][:, :], ACT.Copy).then_inc(s_tern, 1)

            def mix_h(b):
                act.wait_ge(s_ht, b + 1)
                act.activation(h_f, b_ps[:, :], ACT.Identity, bias=beta_c[:, 0:1], scale=gamma_c[:, 0:1])
                act.activation(h_hi[:, :], b_ps[:, :], ACT.Identity, bias=beta_c[:, 0:1], scale=gamma_c[:, 0:1]
                               ).then_inc(s_hhi, 1)

            def mix_z(b, i):
                act.wait_ge(s_z, 2 * b + i + 1)
                act.activation(flat(z_tok[:, 2 * i:2 * i + 2, :]), y_ps[i][:, :], ACT.Silu).then_inc(s_ztok, 1)

            def mix_u(b, h):
                act.wait_ge(s_conv, HALVES * TAPS * b + HALVES * (TAPS - 1) + h + 1)
                act.activation(u[:, h, :], conv[:, h, :], ACT.Silu).then_inc(s_u, 1)

            def mix_xd(b):
                act.wait_ge(s_xdbl, b + 1)
                act.activation(xd[:, :], b_ps[:, :], ACT.Copy).then_inc(s_xdhi, 1)

            def mix_softplus(b):
                for h in range(HALVES):
                    act.wait_ge(s_dtp, HALVES * b + h + 1)
                    act.activation(sp_relu[:, h, :], dA[:, h, :], ACT.Relu, bias=b_dt_c[:, h:h + 1])
                    act.activation(sp_abs[:, h, :], dA[:, h, :], ACT.Abs, bias=b_dt_c[:, h:h + 1]
                                   ).then_inc(s_sparg, 1)
                act.wait_ge(s_sparg, HALVES * b + HALVES)
                act.activation(sp_abs, sp_abs, ACT.Exp, scale=-1.0).then_inc(s_spexp, 1)
                act.wait_ge(s_spexp, b + 1)
                act.activation(sp_abs, sp_abs, ACT.Ln, bias=1.0).then_inc(s_spln, 1)

            def mix_b(b, n):
                act.wait_ge(s_bps, STATE * b + n + 1)
                if n >= 2:
                    act.wait_ge(s_inflow, STATE * b + n - 1)
                act.activation(b_all[:, n % 2, :], b_ps[:, :], ACT.Copy).then_inc(s_ball, 1)

            def mix_decay(b, n):
                if n == 0:
                    act.wait_ge(s_dt, b + 1)
                    act.wait_ge(s_zero, b + 1)
                else:
                    act.wait_ge(s_scan, STATE * b + n)
                act.activation(dA[:, 0, :], dt[:, 0, :], ACT.Exp, scale=decay_c[:, 0, n:n + 1])
                act.activation(dA[:, 1, 1:SEQ], dt[:, 1, 1:SEQ], ACT.Exp, scale=decay_c[:, 1, n:n + 1]
                               ).then_inc(s_dA, 1)

            def mix_gated(b, h):
                act.wait_ge(s_gt, HALVES * b + h + 1)
                act.activation(gated[:, h, :], dA[:, h, :], ACT.Copy).then_inc(s_gated, 1)

            def mix(b, s):
                n = s - SCAN
                if s == 2:
                    mix_h(b)
                if s == 4:
                    mix_z(b, 0)
                    mix_z(b, 1)
                    mix_u(b, 0)
                    mix_u(b, 1)
                    mix_xd(b)
                if s == 5:
                    mix_softplus(b)
                    mix_b(b, 0)
                    mix_b(b, 1)
                    mix_decay(b, 0)
                if 0 <= n < STATE - 1:
                    mix_decay(b, n + 1)
                if 0 <= n < STATE - 2:
                    mix_b(b, n + 2)
                if s == BACK + 1:
                    mix_gated(b, 0)
                    mix_gated(b, 1)

            def norm_hi(i, m):
                p = {1: "a.norm1", 2: "a.norm2", 3: "b.norm3"}[m]
                full(act, i, p)
                act.activation(n_hi[m][:, :], work_of(p)[:, :], ACT.Copy).then_inc(s_nhi[m], 1)

            def ffn_gelu(i, c, j):
                p = c + ".up%d" % j
                full(act, i, p)
                act.activation(gelu[c][:, j, :], work_of(p)[:, :], ACT.Gelu).then_inc(*emptied(p))

            def ffn_square(i, c, j):
                evacuated(act, i, c + ".up%d" % j)
                act.activation(square[c][:, j, :], gelu[c][:, j, :], ACT.Square).then_inc(s_sq[c], 1)

            def gru_in(i, j):
                p = "b.in%d" % j
                full(act, i, p)
                if j < FB:
                    act.activation(in_f[:, j, :], work_of(p)[:, :], ACT.Silu, bias=b1_c[:, j:j + 1])
                    act.activation(in_hi[:, j, :], work_of(p)[:, :], ACT.Silu, bias=b1_c[:, j:j + 1]
                                   ).then_inc(*emptied(p))
                else:
                    act.activation(skip_f[:, j - FB, :], work_of(p)[:, :], ACT.Silu, bias=b2_c[:, j - FB:j - FB + 1]
                                   ).then_inc(*emptied(p))

            def gru_gate(i, j):
                p = "b.z%d" % j
                full(act, i, p)
                if j >= 2:
                    evacuated(act, i, "b.h%d" % (j - 2))
                act.activation(gate[:, j % 2, :], work_of(p)[:, :], ACT.Tanh, scale=0.5, bias=bzh_c[:, j:j + 1]
                               ).then_inc(*emptied(p))

            def a(i, t, s):
                if s == 2:
                    norm_hi(i, 1)
                if s == 3:
                    for j in range(FB):
                        ffn_gelu(i, "a", j)
                    for j in range(FB):
                        ffn_square(i, "a", j)
                if s == 15:
                    norm_hi(i, 2)

            def b(i, t, s):
                if s in (0, 1):
                    for j in range(4 * s, 4 * s + 4):
                        gru_in(i, j)
                if s in GATE_EVAC:
                    gru_gate(i, GATE_EVAC.index(s))
                if s == 21:
                    norm_hi(i, 3)

            def c(i, t, s):
                if s == 3:
                    act.wait_ge(s_inlo, FB * (min(t + 2, ROWS) if isinstance(t, int) else t + 2))
                    for j in range(FB):
                        ffn_gelu(i, "c", j)
                    for j in range(FB):
                        ffn_square(i, "c", j)

            act.wait_ge(s_w_mix, W_MIX)
            act.activation(decay_c[:, :, :], decay_c[:, :, :], ACT.Exp).then_inc(s_expA, 1)
            rounds(act, mix, a, b, c, prepare)

        @block.vector
        def _(dve):
            def prepare_mix():
                dve.wait_ge(s_eye, 2)
                dve.tensor_tensor(pick[:, :], ident[:, 0:2 * STATE], ident[:, 2 * STATE:4 * STATE], ALU.add
                                  ).then_inc(s_pick, 1)
                dve.wait_ge(s_w_mix, W_MIX)
                dve.tensor_copy(win_hi[:, :], win_f).then_inc(s_win_hi, 1)
                dve.tensor_copy(wdt_hi[:, :], wdt_f[:, :]).then_inc(s_wdt_hi, 1)
                dve.wait_ge(s_win_hi, 1)
                dve.tensor_tensor(win_lo[:, :], win_f, win_hi[:, :].bitcast(F32), ALU.subtract).then_inc(s_win, 1)
                dve.wait_ge(s_wdt_hi, 1)
                dve.tensor_tensor(wdt_lo[:, :], wdt_f[:, :], wdt_hi[:, :].bitcast(F32), ALU.subtract
                                  ).then_inc(s_wdt, 1)
                dve.wait_ge(s_expA, 1)
                dve.tensor_scalar(decay_c[:, :, :], decay_c[:, :, :], -1.0, None, ALU.mult).then_inc(s_A, 1)

            def prepare(i, s):
                if (i, s) == (0, SCAN + 2):
                    dve.wait_ge(s_w_tail, W_TAIL)
                    dve.tensor_reduce(abs_sum[:, 0:1], flat(up_raw[:, :, :]), AX_X, ALU.add,
                                      apply_absolute_value=True).then_inc(s_abs, 1)
                    dve.tensor_reduce(abs_sum[:, 1:2], down_raw, AX_X, ALU.add, apply_absolute_value=True
                                      ).then_inc(s_abs, 1)
                if (i, s) == (0, SCAN + 4):
                    dve.wait_ge(s_abs_all, 1)
                    dve.tensor_scalar(thr[:, :], work[0][:, 0:2], 0.5 / (FF * D), None, ALU.mult).then_inc(s_thr, 1)
                    dve.tensor_scalar(thr_neg[:, :], work[0][:, 0:2], -0.5 / (FF * D), None, ALU.mult
                                      ).then_inc(s_thr, 1)
                    dve.wait_ge(s_thr, 2)
                if (i, s) in ((0, SCAN + 5), (0, SCAN + 7)):
                    k = (s - SCAN - 5) // 2
                    raw, sign = ((flat(up_raw[:, :, :]), flat(up_sign[:, :, :])), (down_raw, down_sign))[k]
                    dve.tensor_scalar(below, raw, thr_neg[:, k:k + 1], None, ALU.is_lt).then_inc(s_below, 1)
                    dve.wait_ge(s_below, k + 1)
                    dve.scalar_tensor_tensor(sign, raw, thr[:, k:k + 1], below, ALU.is_gt, ALU.subtract
                                             ).then_inc(s_sign, 1)
                    dve.wait_ge(s_sign, k + 1)

            def mix_norm(b):
                dve.wait_ge(s_x_in, 16 * b + 16)
                for j in range(TILES):
                    last = dve.bn_stats(m_stat[:, j, :], x_tok[:, j, :])
                last.then_inc(s_mstat, 1)
                dve.wait_ge(s_mstat, b + 1)
                dve.sem_inc(s_passed)
                for j in range(TILES):
                    last = dve.bn_aggr(m_mv[:, j, :], m_stat[:, j, :])
                last.then_inc(s_mmv, 1)
                dve.wait_ge(s_mmv, b + 1)
                dve.tensor_scalar(m_vv[:, 0, :], m_mv[:, :, 1], LN_EPS, None, ALU.add)
                dve.tensor_scalar(m_vv[:, 1, :], m_mv[:, :, 1], 1.0 + LN_EPS, LN_EPS * LN_EPS, ALU.mult, ALU.add
                                  ).then_inc(s_mvv, 1)

            def mix_apply(b):
                dve.wait_ge(s_mroot, b + 1)
                wait(dve, s_base, b)
                dve.tensor_scalar(m_gain[:, :], m_root[:, 0, :], 1.0, None, ALU.add).then_inc(s_mgs, 1)
                dve.scalar_tensor_tensor(m_shift[:, :], m_mv[:, :, 0], -1.0, m_root[:, 0, :], ALU.mult, ALU.mult
                                         ).then_inc(s_mgs, 1)
                wait(dve, s_hlo, b)
                for j in range(TILES):
                    last = dve.tensor_scalar(h_tok[:, j, :], x_tok[:, j, :], m_mv[:, j, 0:1], m_root[:, 1, j:j + 1],
                                             ALU.subtract, ALU.mult)
                last.then_inc(s_htok, 1)

            def mix_conv(b):
                wait(dve, s_acc, STATE * b)
                for s in range(TAPS):
                    for h in range(HALVES):
                        w = taps_c[:, h, TAPS - 1 - s:TAPS - s]
                        if s == 0:
                            dve.wait_ge(s_xi, HALVES * b + h + 1)
                            dve.tensor_scalar(conv[:, h, :], dA[:, h, :], w, b_conv_c[:, h:h + 1], ALU.mult, ALU.add
                                              ).then_inc(s_conv, 1)
                        else:
                            dve.wait_ge(s_conv, HALVES * TAPS * b + HALVES * (s - 1) + h + 1)
                            dve.scalar_tensor_tensor(conv[:, h, s:SEQ], dA[:, h, 0:SEQ - s], w, conv[:, h, s:SEQ],
                                                     ALU.mult, ALU.add).then_inc(s_conv, 1)

            def mix_skip(b):
                dve.wait_ge(s_u, HALVES * b + HALVES)
                for h in range(HALVES):
                    last = dve.tensor_scalar(skip_u[:, h, :], u[:, h, :], skip_c[:, h:h + 1], None, ALU.mult)
                last.then_inc(s_skip, 1)

            def mix_xd_lo(b):
                dve.wait_ge(s_xdhi, b + 1)
                for q in (32, 96):
                    last = dve.tensor_tensor(xd[q:q + 32, :], b_ps[q:q + 32, :], xd[q:q + 32, :].bitcast(F32),
                                             ALU.subtract)
                last.then_inc(s_xdlo, 1)

            def mix_zero(b):
                dve.wait_ge(s_sparg, HALVES * b + HALVES)
                dve.tensor_scalar(dA[:, 1, 0:1], ones[:, 0:1], 0.0, None, ALU.mult).then_inc(s_zero, 1)

            def mix_scan(b, n):
                dve.wait_ge(s_dA, STATE * b + n + 1)
                dve.wait_ge(s_inflow, STATE * b + n + 1)
                if n >= 3:
                    dve.wait_ge(s_acc, STATE * b + n - 2)
                dve.tensor_tensor_scan(flat(state[:, n % 3, :, :]), flat(dA[:, :, :]), flat(inflow[:, n % 2, :, :]),
                                       0.0, ALU.mult, ALU.add).then_inc(s_scan, 1)

            def mix_read(b, n):
                dve.wait_ge(s_scan, STATE * b + n + 1)
                dve.wait_ge(s_cps, STATE * b + n + 1)
                dve.tensor_tensor(state[:, n % 3, :, :], state[:, n % 3, :, :],
                                  c_ps[:, :].unsqueeze(1).broadcast_to([P, HALVES, SEQ]), ALU.mult
                                  ).then_inc(s_read, 1)

            def mix_gate(b):
                dve.wait_ge(s_acc, STATE * b + STATE)
                dve.wait_ge(s_ztok, 2 * b + 2)
                for i in range(2):
                    at = flat(z_tok[:, 2 * i:2 * i + 2, :])
                    dve.tensor_tensor(at, y_ps[i][:, :], at, ALU.mult).then_inc(s_gtok, 1)

            def mix_x1(b):
                dve.wait_ge(s_mix, b + 1)
                dve.wait_ge(s_base, b + 1)
                dve.tensor_tensor(flat(x1_tok[:, :, :]), b_ps[:, :], flat(base_tok[:, :, :]), ALU.add
                                  ).then_inc(s_x1, 1)

            def mix(b, s):
                n = s - SCAN
                if s == 0:
                    mix_norm(b)
                if s == 1:
                    mix_apply(b)
                if s == 3:
                    mix_conv(b)
                if s == 4:
                    mix_skip(b)
                    mix_xd_lo(b)
                if s == 5:
                    mix_zero(b)
                if 0 <= n < STATE:
                    mix_scan(b, n)
                if 1 <= n <= STATE:
                    mix_read(b, n - 1)
                if s == BACK:
                    mix_gate(b)
                if s == BACK + 1:
                    mix_x1(b)

            def norm_stats(t, m, src):
                for j in range(TILES):
                    last = dve.bn_stats(stat[m][:, j, :], src[:, j, :])
                last.then_inc(s_stat[m], 1)
                dve.wait_ge(s_stat[m], t + 1)
                dve.sem_inc(s_passed)
                for j in range(TILES):
                    last = dve.bn_aggr(mv[m][:, j, :], stat[m][:, j, :])
                last.then_inc(s_mv[m], 1)
                dve.wait_ge(s_mv[m], t + 1)
                for k, eps in enumerate((LN_EPS, LN_EPS) if m == 2 else (0.0, LN_EPS)):
                    last = dve.tensor_scalar(vv[m][:, k, :], mv[m][:, :, 1], eps, None, ALU.add)
                last.then_inc(s_vv[m], 1)

            def norm_apply(t, m, src):
                dve.wait_ge(s_root[m], t + 1)
                by = root[m][:, 0, :]
                if m != 2:
                    dve.scalar_tensor_tensor(den[m][:, :], root[m][:, 1, :], RMS_EPS, root[m][:, 0, :],
                                             ALU.mult, ALU.add).then_inc(s_den[m], 1)
                    dve.wait_ge(s_den[m], t + 1)
                    dve.reciprocal(scale[m][:, :], den[m][:, :]).then_inc(s_scale[m], 1)
                    dve.wait_ge(s_scale[m], t + 1)
                    by = scale[m]
                for j in range(TILES):
                    last = dve.tensor_scalar(n_tok[m][:, j, :], src[:, j, :], mv[m][:, j, 0:1], by[:, j:j + 1],
                                             ALU.subtract, ALU.mult)
                last.then_inc(s_ntok[m], 1)

            def norm_lo(i, t, m):
                p = {1: "a.norm1", 2: "a.norm2", 3: "b.norm3"}[m]
                dve.wait_ge(s_nhi[m], t + 1)
                dve.tensor_tensor(n_lo[m][:, :], work_of(p)[:, :], n_hi[m][:, :].bitcast(F32), ALU.subtract
                                  ).then_inc(*emptied(p))

            def ffn_ms(i, c):
                p = c + ".sumsq"
                full(dve, i, p)
                dve.tensor_scalar(ms[c][:, :], work_of(p)[:, 0:TILES], 1.0 / FF, None, ALU.mult
                                  ).then_inc(*emptied(p))

            def ffn_out(i, t, c, src, dst):
                p = c + ".down"
                dve.wait_ge(s_rms[c], t + 1)
                dve.tensor_scalar(rden[c][:, :], rms[c][:, :], RMS_EPS, None, ALU.add).then_inc(s_rden[c], 1)
                dve.wait_ge(s_rden[c], t + 1)
                dve.reciprocal(rscale[c][:, :], rden[c][:, :]).then_inc(s_rscale[c], 1)
                dve.wait_ge(s_rscale[c], t + 1)
                full(dve, i, p)
                for j in range(TILES):
                    last = dve.scalar_tensor_tensor(dst[:, j, :], work_of(p)[:, cols(j)], rscale[c][:, j:j + 1],
                                                    src[:, j, :], ALU.mult, ALU.add)
                last.then_inc(*emptied(p))

            def gru_new(i, t, j):
                p = "b.h%d" % j
                full(dve, i, p)
                dve.wait_ge(s_gate1, FB * t + j + 1)
                if j >= 2:
                    dve.wait_ge(s_mixed, FB * t + j - 1)
                dve.scalar_tensor_tensor(hid[:, j % 2, :], work_of(p)[:, :], bh_c[:, j:j + 1], gate[:, j % 2, :],
                                         ALU.add, ALU.mult).then_inc(*emptied(p))

            def gru_scan(i, t, j):
                evacuated(dve, i, "b.h%d" % j)
                dve.wait_ge(s_keep, FB * t + j + 1)
                dve.tensor_tensor_scan(hid[:, j % 2, :], keep[:, j % 2, :], hid[:, j % 2, :], 0.0,
                                       ALU.mult, ALU.add).then_inc(s_hid, 1)

            def gru_mixed(t, j):
                dve.wait_ge(s_hid, FB * t + j + 1)
                dve.scalar_tensor_tensor(mixed[:, j, :], hid[:, j % 2, :], 0.5, skip_f[:, j, :], ALU.mult, ALU.add
                                         ).then_inc(s_mixed, 1)

            def gru_out(i, t):
                full(dve, i, "b.out")
                dve.wait_ge(s_x2b, t + 1)
                dve.wait_ge(s_out, 16 * t + 16)
                dve.tensor_tensor(flat(x3_tok[:, :, :]), work_of("b.out")[:, :], flat(x2b_tok[:, :, :]), ALU.add
                                  ).then_inc(*emptied("b.out"))

            def a(i, t, s):
                if s == 0:
                    dve.wait_ge(s_x1, t + 1)
                    norm_stats(t, 1, x1_tok)
                if s == 1:
                    norm_apply(t, 1, x1_tok)
                if s == 2:
                    norm_lo(i, t, 1)
                if s == 5:
                    ffn_ms(i, "a")
                if s == 9:
                    ffn_out(i, t, "a", x1_tok, x2_tok)
                    evacuated(dve, i, "a.down")
                    norm_stats(t, 2, x2_tok)
                if s == 10:
                    norm_apply(t, 2, x2_tok)
                if s == 15:
                    norm_lo(i, t, 2)

            def b(i, t, s):
                if s in NEW_EVAC:
                    j = NEW_EVAC.index(s)
                    gru_new(i, t, j)
                    gru_scan(i, t, j)
                    gru_mixed(t, j)
                if s == 20:
                    gru_out(i, t)
                    evacuated(dve, i, "b.out")
                    norm_stats(t, 3, x3_tok)
                if s == 21:
                    norm_apply(t, 3, x3_tok)
                    norm_lo(i, t, 3)

            def c(i, t, s):
                if s == 5:
                    ffn_ms(i, "c")
                if s == 12:
                    ffn_out(i, t, "c", x3_tok, out_tok)

            dve.wait_ge(s_const, 3)
            prepare_mix()
            rounds(dve, mix, a, b, c, prepare)

        @block.tensor
        def _(pe):
            def three(dst, w_hi, w_lo, r_hi, r_lo, start=True, stop=True):
                pe.matmul(dst, w_hi, r_hi, start=start, stop=False)
                pe.matmul(dst, w_lo, r_hi, start=False, stop=False)
                return pe.matmul(dst, w_hi, r_lo, start=False, stop=stop)

            def prepare(i, s):
                if (i, s) == (0, SCAN + 3):
                    pe.wait_ge(s_abs, 2)
                    pe.matmul(work[0][:, 0:2], ones[:, :], abs_sum[:, :], start=True, stop=True
                              ).then_inc(s_abs_all, 1)
                if (i, s) == (0, SCAN + 10):
                    pe.wait_ge(s_sign, 1)
                    for k in range(FB):
                        last = pe.transpose(work[0][:, cols(k)], up_sign[:, k, :], ident[:, :])
                    last.then_inc(s_tern_t, 1)
                    pe.wait_ge(s_sign, 2)
                    for k in range(FB):
                        last = pe.transpose(work[1][:, cols(k)], down_sign[:, cols(k)], ident[:, :])
                    last.then_inc(s_tern_t, 1)
                if (i, s) == (0, SLOTS - 1):
                    pe.wait_ge(s_tern, 2)
                    pe.wait_ge(s_lo12, 1)
                    pe.wait_ge(s_lozh, FB)

            def mix_ht(b):
                pe.wait_ge(s_htok, b + 1)
                wait(pe, s_x1, b)
                for j in range(TILES):
                    last = pe.transpose(b_ps[:, cols(j)], h_tok[:, j, :], ident[:, :])
                last.then_inc(s_ht, 1)

            def mix_in(b):
                pe.wait_ge(s_hhi, b + 1)
                pe.wait_ge(s_hlo, b + 1)
                wait(pe, s_gated, HALVES * b)
                for h in range(HALVES):
                    three(dA[:, h, :], win_hi[:, cols(h)], win_lo[:, cols(h)], h_hi[:, :], h_lo[:, :]
                          ).then_inc(s_xi, 1)

            def mix_zin(b):
                for i in range(2):
                    for j in (2 * i, 2 * i + 1):
                        at = slice((j % 2) * INNER, (j % 2 + 1) * INNER)
                        last = three(y_ps[i][:, at], h_hi[:, cols(j)], h_lo[:, cols(j)],
                                     win_hi[:, INNER:2 * INNER], win_lo[:, INNER:2 * INNER])
                    last.then_inc(s_z, 1)

            def mix_xdbl(b):
                pe.wait_ge(s_u, HALVES * b + HALVES)
                for h in range(HALVES):
                    last = pe.matmul(b_ps[:, :], wx_rep[:, h, :], u[:, h, :], start=(h == 0), stop=(h == HALVES - 1))
                last.then_inc(s_xdbl, 1)

            def mix_dtp(b):
                pe.wait_ge(s_xdlo, b + 1)
                for h in range(HALVES):
                    pe.matmul(dA[:, h, :], wdt_hi[:, cols(h)], xd[:, :], start=True, stop=False)
                    pe.matmul(dA[:, h, :], wdt_lo[:, cols(h)], xd[:, :], start=False, stop=True).then_inc(s_dtp, 1)

            def y_region(j, h):
                at = (j % 2) * INNER + h * P
                return y_ps[j // 2][:, at:at + P]

            def mix_skip(b):
                pe.wait_ge(s_skip, b + 1)
                pe.wait_ge(s_ztok, 2 * b + 2)
                for j in range(TILES):
                    for h in range(HALVES):
                        last = pe.matmul(y_region(j, h), skip_u[:, h, cols(j)], ident[:, :], is_transpose=True,
                                         start=(j % 2 == 0 and h == 0), stop=False, skip_group_check=True)
                last.then_inc(s_y0, 1)

            def mix_bn(b, n):
                if n:
                    pe.wait_ge(s_ball, STATE * b + n)
                pe.matmul(b_ps[:, :], pick[:, n:n + 1].broadcast_to([P, P]), xd[:, :], start=True, stop=True).then_inc(s_bps, 1)

            def mix_cn(b, n):
                if n:
                    pe.wait_ge(s_read, STATE * b + n)
                pe.matmul(c_ps[:, :], pick[:, STATE + n:STATE + n + 1].broadcast_to([P, P]), xd[:, :], start=True, stop=True).then_inc(s_cps, 1)

            def mix_acc(b, n):
                pe.wait_ge(s_read, STATE * b + n + 1)
                for h in range(HALVES):
                    for j in range(TILES):
                        last = pe.matmul(y_region(j, h), state[:, n % 3, h, cols(j)], ident[:, :], is_transpose=True,
                                         start=False, stop=(n == STATE - 1), skip_group_check=True)
                last.then_inc(s_acc, 1)

            def mix_out(b):
                pe.wait_ge(s_gtok, 2 * b + 2)
                for h in range(HALVES):
                    for j in range(TILES):
                        last = pe.transpose(dA[:, h, cols(j)], gated_tok[:, j, cols(h)], ident[:, :])
                    last.then_inc(s_gt, 1)
                pe.wait_ge(s_gated, HALVES * b + HALVES)
                for j in range(TILES):
                    for h in range(HALVES):
                        last = pe.matmul(b_ps[:, cols(j)], gated[:, h, cols(j)], wout_sb[:, h, :],
                                         start=(h == 0), stop=(h == HALVES - 1))
                last.then_inc(s_mix, 1)

            def mix(b, s):
                n = s - SCAN
                if s == 1:
                    mix_ht(b)
                if s == 3:
                    mix_in(b)
                    mix_zin(b)
                if s == 4:
                    mix_xdbl(b)
                if s == 5:
                    mix_dtp(b)
                    mix_skip(b)
                    mix_bn(b, 0)
                    mix_bn(b, 1)
                    mix_cn(b, 0)
                if 1 <= n <= STATE:
                    if n < STATE:
                        mix_cn(b, n)
                    mix_acc(b, n - 1)
                if 0 <= n < STATE - 2:
                    mix_bn(b, n + 2)
                if s == BACK + 1:
                    mix_out(b)

            def norm_t(i, t, m):
                p = {1: "a.norm1", 2: "a.norm2", 3: "b.norm3"}[m]
                pe.wait_ge(s_ntok[m], t + 1)
                bank_free(pe, i, p)
                for j in range(TILES):
                    last = pe.transpose(work_of(p)[:, cols(j)], n_tok[m][:, j, :], ident[:, :])
                last.then_inc(*made(p))

            def ffn_up(i, c, j):
                p = c + ".up%d" % j
                m = {"a": 1, "c": 3}[c]
                if j == 0:
                    if c == "a":
                        evacuated(pe, i, "a.norm1")
                    else:
                        evacuated(pe, i - 1, "b.norm3")
                bank_free(pe, i, p)
                pe.matmul(work_of(p)[:, :], up_t[:, cols(j)], n_hi[m][:, :], start=True, stop=False)
                pe.matmul(work_of(p)[:, :], up_t[:, cols(j)], n_lo[m][:, :], start=False, stop=True
                          ).then_inc(*made(p))

            def ffn_down(i, c, part):
                p = c + ".down"
                if part == 0:
                    evacuated(pe, i, c + ".up2")
                    evacuated(pe, i, c + ".up3")
                    bank_free(pe, i, p)
                for k in range(FB):
                    last = pe.matmul(work_of(p)[:, cols(part)], gelu[c][:, k, cols(part)], down_t[:, k, :],
                                     start=(k == 0), stop=(k == FB - 1))
                if part == TILES - 1:
                    last.then_inc(*made(p))

            def ffn_sumsq(i, t, c):
                p = c + ".sumsq"
                pe.wait_ge(s_sqsum[c], t + 1)
                bank_free(pe, i, p)
                for j in range(TILES):
                    last = pe.matmul(work_of(p)[:, j:j + 1], sq_sum[c][:, cols(j)], ones[:, 0:1],
                                     start=True, stop=True)
                last.then_inc(*made(p))

            def gru_in(i, j):
                p = "b.in%d" % j
                if j == 0:
                    evacuated(pe, i - 1, "a.norm2")
                bank_free(pe, i, p)
                three(work_of(p)[:, :], w12_hi[:, cols(j)], w12_lo[:, cols(j)], n_hi[2][:, :], n_lo[2][:, :]
                      ).then_inc(*made(p))

            def gru_gate(i, t, which, j, k):
                p = "b.%s%d" % (which, j)
                if p == "b.z0":
                    pe.wait_ge(s_inlo, FB * t + k + 1)
                if k == 0:
                    bank_free(pe, i, p)
                at = (which == "h") * FF + j * P
                last = three(work_of(p)[:, :], wzh_hi[:, k, at:at + P], wzh_lo[:, k, at:at + P],
                             in_hi[:, k, :], in_lo[:, k, :], start=(k == 0), stop=(k == FB - 1))
                if k == FB - 1:
                    last.then_inc(*made(p))

            def gru_out(i, t, part):
                p = "b.out"
                if part == 0:
                    pe.wait_ge(s_mixed, FB * t + FB)
                    bank_free(pe, i, p)
                for k in range(FB):
                    last = pe.matmul(work_of(p)[:, cols(part)], mixed[:, k, cols(part)], wo_sb[:, k, :],
                                     start=(k == 0), stop=(k == FB - 1))
                if part == TILES - 1:
                    last.then_inc(*made(p))

            GATES_AT = {3: ("z", 0, (0, 1, 2, 3)), 5: ("h", 0, (0, 1, 2, 3)), 6: ("z", 1, (0, 1, 2, 3)),
                        8: ("h", 1, (0, 1)), 9: ("h", 1, (2, 3)), 11: ("z", 2, (0, 1)), 12: ("z", 2, (2, 3)),
                        13: ("h", 2, (0, 1, 2, 3)), 14: ("z", 3, (0, 1, 2, 3)), 16: ("h", 3, (0, 1, 2, 3))}

            def a(i, t, s):
                if s == 2:
                    norm_t(i, t, 1)
                if s == 3:
                    for j in range(FB):
                        ffn_up(i, "a", j)
                if s == 5:
                    ffn_sumsq(i, t, "a")
                if s in (7, 8):
                    ffn_down(i, "a", 2 * (s - 7))
                    ffn_down(i, "a", 2 * (s - 7) + 1)
                if s == 15:
                    norm_t(i, t, 2)

            def b(i, t, s):
                if s in (0, 1):
                    for j in range(4 * s, 4 * s + 4):
                        gru_in(i, j)
                if s in GATES_AT:
                    which, j, blocks = GATES_AT[s]
                    for k in blocks:
                        gru_gate(i, t, which, j, k)
                if s in (18, 19):
                    gru_out(i, t, 2 * (s - 18))
                    gru_out(i, t, 2 * (s - 18) + 1)
                if s == 21:
                    norm_t(i, t, 3)

            def c(i, t, s):
                if s == 3:
                    for j in range(FB):
                        ffn_up(i, "c", j)
                if s == 5:
                    ffn_sumsq(i, t, "c")
                if s in (10, 11):
                    ffn_down(i, "c", 2 * (s - 10))
                    ffn_down(i, "c", 2 * (s - 10) + 1)

            pe.wait_ge(s_const, 3)
            pe.wait_ge(s_eye, 2)
            pe.wait_ge(s_win, 1)
            pe.wait_ge(s_wdt, 1)
            pe.wait_ge(s_pick, 1)
            pe.wait_ge(s_A, 1)
            rounds(pe, mix, a, b, c, prepare)


_INS = ["x", "gamma", "beta", "W_in", "W_conv", "b_conv", "W_x", "W_dt", "b_dt", "A_log", "Dskip", "W_out",
        "W1", "b1", "W2", "b2", "Wz", "bz", "Wh", "bh", "Wo", "bo", "w_up", "w_down"]


def kernel(**inputs):
    import numpy as np
    import concourse.bacc as bacc
    from concourse import mybir
    from concourse.bass_utils import run_bass_kernel_spmd

    nc = bacc.Bacc("TRN2", target_bir_lowering=False, num_devices=1)
    short = {}
    for name, a in inputs.items():
        for prefix in ("L0_attn_a_", "L0_attn_b_", "L0_ffn_"):
            if name.startswith(prefix):
                short[name[len(prefix):]] = np.ascontiguousarray(a)
    arrays, args = {}, []
    for name in _INS:
        a = short[name]
        arrays[f"in_{name}"] = a
        args.append(nc.dram_tensor(f"in_{name}", a.shape, mybir.dt.from_np(a.dtype), kind="ExternalInput").ap())
    x = short["x"]
    args.append(nc.dram_tensor("out_x", x.shape, mybir.dt.from_np(x.dtype), kind="ExternalOutput").ap())
    build(nc, *args)
    r = run_bass_kernel_spmd(nc, [arrays], core_ids=[0])
    return r.results[0]["out_x"]
```

```python
from contextlib import ExitStack

import concourse.bass as bass
from concourse import mybir

F32 = mybir.dt.float32
F32R = mybir.dt.float32r
ALU = mybir.AluOpType
ACT = mybir.ActivationFunctionType
AX_X = mybir.AxisListType.X

P = 128
ROWS, SEQ, D = 8, 512, 128
TILES = SEQ // P
INNER = 256
HALVES = INNER // P
STATE = 16
TAPS = 4
RANK = 8
FF = 512
FB = FF // P
LN_EPS = 1e-5
RMS_EPS = 1e-8

SCAN = 4
BACK = SCAN + STATE
SLOTS = BACK + 4
GATE_SLOTS, KEEP_SLOTS, NEW_SLOTS, HID_SLOTS = (3, 5, 7, 9), (4, 6, 8, 10), (4, 6, 8, 11), (5, 7, 9, 12)
LAG = {"a": 1, "b": 2, "c": 3}
FIRST_FULL = 3
ROUNDS = ROWS + 3

BANKS = (["b.in6", "c.up1", "c.up3", "a.up1", "a.up3", "b.h0", "b.h1", "b.h2", "c.sumsq",
          "c.down", "a.sumsq", "a.down", "a.norm2", "a.in0", "a.in2", "a.in4"],
         ["b.in7", "c.up0", "c.up2", "a.up0", "a.up2", "b.z0", "b.z1", "b.z2", "b.z3", "b.h3",
          "b.out", "b.norm3", "a.in1", "a.in3", "a.in5"])
WORK_BANK = {p: k for k in range(2) for p in BANKS[k]}


def mark(i, product):
    def there(r):
        return [p for p in BANKS[WORK_BANK[product]] if LAG[p[0]] <= r < LAG[p[0]] + ROWS]
    if isinstance(i, int):
        return sum(len(there(r)) for r in range(i)) + there(i).index(product) + 1
    every = there(FIRST_FULL)
    before = sum(len(there(r)) for r in range(FIRST_FULL))
    return (i - FIRST_FULL) * len(every) + before + every.index(product) + 1


def build(nc, x, gamma, beta, W_in, W_conv, b_conv, W_x, W_dt, b_dt, A_log, Dskip, W_out,
          W1, b1, W2, b2, Wz, bz, Wh, bh, Wo, bo, w_up, w_down, out):
    ctx = ExitStack()
    with ctx:
        def sb(name, shape, dt=F32):
            return ctx.enter_context(nc.sbuf_tensor(name, shape, dt))

        def sem(name):
            return ctx.enter_context(nc.semaphore(name))

        def flat(a):
            return a.rearrange("p a b -> p (a b)")

        ident = sb("ident", [P, P])
        ones = sb("ones", [P, P])
        minus_half = sb("minus_half", [P, 8])
        plus_half = sb("plus_half", [P, 8])
        pick = sb("pick", [P, 2 * STATE], F32R)
        gamma_c, beta_c = sb("gamma_c", [P, 1]), sb("beta_c", [P, 1])
        taps_c = sb("taps_c", [P, HALVES, TAPS])
        b_conv_c, b_dt_c = sb("b_conv_c", [P, HALVES]), sb("b_dt_c", [P, HALVES])
        skip_c = sb("skip_c", [P, HALVES])
        decay_c = sb("decay_c", [P, HALVES, STATE])
        win_hi, win_lo = sb("win_hi", [P, 2 * INNER], F32R), sb("win_lo", [P, 2 * INNER], F32R)
        wx_rep = sb("wx_rep", [P, HALVES, P])
        wdt_f = sb("wdt_f", [P, INNER])
        wdt_hi, wdt_lo = sb("wdt_hi", [P, INNER], F32R), sb("wdt_lo", [P, INNER], F32R)
        wout_sb = sb("wout_sb", [P, HALVES, D])
        w12_hi, w12_lo = sb("w12_hi", [P, 2 * FF], F32R), sb("w12_lo", [P, 2 * FF], F32R)
        wzh_hi = sb("wzh_hi", [P, FB, 2 * FF], F32R)
        wzh_lo = sb("wzh_lo", [P, FB, 2 * FF], F32R)
        wo_sb = sb("wo_sb", [P, FB, D])
        b1_c, b2_c, bz_c, bh_c = (sb(n, [P, FB]) for n in ("b1_c", "b2_c", "bz_c", "bh_c"))
        bzh_c = sb("bzh_c", [P, FB])
        bo_tok = sb("bo_tok", [P, TILES, D])
        up_t = sb("up_t", [P, FF], F32R)
        down_t = sb("down_t", [P, FB, D])
        abs_sum = sb("abs_sum", [P, 2])
        thr, thr_neg = sb("thr", [P, 2]), sb("thr_neg", [P, 2])

        x_tok = sb("x_tok", [P, TILES, D])
        m_stat, m_mv = sb("m_stat", [P, TILES, 6]), sb("m_mv", [P, TILES, 2])
        m_vv, m_root = sb("m_vv", [P, 2, TILES]), sb("m_root", [P, 2, TILES])
        m_gain, m_shift = sb("m_gain", [P, TILES]), sb("m_shift", [P, TILES])
        h_tok = sb("h_tok", [P, TILES, D])
        h_f = flat(h_tok[:, :, :])
        base_tok = sb("base_tok", [P, TILES, D])
        h_hi, h_lo = sb("h_hi", [P, SEQ], F32R), sb("h_lo", [P, SEQ], F32R)
        u = sb("u", [P, HALVES, SEQ])
        z_tok = sb("z_tok", [P, TILES, INNER])
        xd = sb("xd", [P, SEQ], F32R)
        dt = sb("dt", [P, HALVES, SEQ])
        dtu = sb("dtu", [P, HALVES, SEQ])
        b_all = sb("b_all", [P, 2, SEQ])
        inflow = sb("inflow", [P, 2, HALVES, SEQ])
        state = sb("state", [P, 3, HALVES, SEQ])
        sp_relu = dtu
        conv = sp_abs = state[:, 2, :, :]
        skip_u = inflow[:, 1, :, :]
        gated = inflow[:, 0, :, :]
        gated_tok = z_tok

        x1_tok, x2_tok, x2b_tok = (sb(n, [P, TILES, D]) for n in ("x1_tok", "x2_tok", "x2b_tok"))
        x3_tok = sb("x3_tok", [P, TILES, D])
        out_tok = x3_tok
        NORMS = (1, 2, 3)
        stat = {m: sb("stat%d" % m, [P, TILES, 6]) for m in NORMS}
        mv = {m: sb("mv%d" % m, [P, TILES, 2]) for m in NORMS}
        vv = {m: sb("vv%d" % m, [P, 2, TILES]) for m in NORMS}
        root = {m: sb("root%d" % m, [P, 2, TILES]) for m in NORMS}
        den = {m: sb("den%d" % m, [P, TILES]) for m in NORMS}
        scale = {m: sb("scale%d" % m, [P, TILES]) for m in NORMS}
        n_tok = sb("n_tok", [P, TILES, D])
        n_hi = {m: sb("n_hi%d" % m, [P, SEQ], F32R) for m in NORMS}
        n_lo = {m: sb("n_lo%d" % m, [P, SEQ], F32R) for m in NORMS}
        wide = sb("wide", [P, 2 * FB, SEQ])
        act_b = sb("act_b", [P, FB, SEQ])
        square_c = sb("square_c", [P, FB, SEQ])
        mixed = sb("mixed", [P, FB, SEQ])
        gelu = {"a": wide[:, 0:FB, :], "c": act_b}
        square = {"a": wide[:, FB:2 * FB, :], "c": square_c}
        sq_sum = {"a": wide[:, FB, :], "c": square_c[:, 0, :]}
        ms = {c: sb("ms_" + c, [P, TILES]) for c in "ac"}
        rms = {c: sb("rms_" + c, [P, TILES]) for c in "ac"}
        rden = {c: sb("rden_" + c, [P, TILES]) for c in "ac"}
        rscale = {c: sb("rscale_" + c, [P, TILES]) for c in "ac"}
        in_f = square_c
        in_hi, in_lo = sb("in_hi", [P, FB, SEQ], F32R), sb("in_lo", [P, FB, SEQ], F32R)
        skip_f = sb("skip_f", [P, FB, SEQ])
        gate = sb("gate", [P, 2, SEQ])
        keep = sb("keep", [P, 2, SEQ])
        win_f = dtu[:, 0, :]
        w12_f = flat(skip_f[:, 0:2, :])
        wzh_f = flat(wide[:, :, :]).rearrange("p (k n) -> p k n", k=FB)
        up_raw, up_sign = x2_tok, x2b_tok
        down_raw, down_sign = flat(x3_tok[:, :, :]), flat(x1_tok[:, :, :])
        below = flat(n_tok[:, :, :])

        def pb(name, shape):
            return ctx.enter_context(nc.psum_tensor(name, shape, F32))

        dA = pb("dA", [P, HALVES, SEQ])
        b_ps, c_ps = pb("b_ps", [P, SEQ]), pb("c_ps", [P, SEQ])
        y_ps = [pb("y_ps0", [P, SEQ]), pb("y_ps1", [P, SEQ])]
        work = [pb("work0", [P, SEQ]), pb("work1", [P, SEQ])]

        s_w_mix, s_w_tail, s_w_zh = sem("w_mix"), sem("w_tail"), sem("w_zh")
        s_x_in, s_out = sem("x_in"), sem("out_stored")
        s_const, s_eye = sem("const"), sem("eye")
        s_passed = sem("passed")
        s_pick = sem("pick_ready")
        s_expA, s_A = sem("exp_A"), sem("A_ready")
        s_win_hi, s_win = sem("win_hi_ready"), sem("win_ready")
        s_wdt_hi, s_wdt = sem("wdt_hi_ready"), sem("wdt_ready")
        s_wxz = sem("zeros_ready")
        s_hi12, s_lo12, s_hizh, s_lozh = sem("hi12"), sem("lo12"), sem("hizh"), sem("lozh")
        s_bzh = sem("bzh_ready")
        s_abs, s_abs_all, s_thr, s_below, s_sign = (sem("abs_sums"), sem("abs_all"), sem("thresholds"),
                                                    sem("below_mask"), sem("signs"))
        s_tern_t, s_tern = sem("ternary_transposed"), sem("ternary_ready")

        s_mstat, s_mmv, s_mvv, s_mroot = sem("m_stat_s"), sem("m_mv_s"), sem("m_vv_s"), sem("m_root_s")
        s_mgs, s_htok, s_base = sem("m_gain_shift"), sem("h_tok_ready"), sem("base_ready")
        s_ht, s_hhi, s_hlo = sem("h_transposed"), sem("h_hi_ready"), sem("h_lo_ready")
        s_xi, s_z, s_ztok = sem("xi_full"), sem("z_full"), sem("z_tok_ready")
        s_conv, s_u, s_skip, s_y0 = sem("conv_steps"), sem("u_ready"), sem("skip_ready"), sem("y_started")
        s_xdbl, s_xdhi, s_xdlo = sem("xdbl_full"), sem("xd_hi_ready"), sem("xd_lo_ready")
        s_dtp, s_sparg, s_spexp, s_spln = (sem("dt_full"), sem("softplus_args"), sem("softplus_exp"),
                                           sem("softplus_ln"))
        s_relu = sem("relu_ready")
        s_inhi = sem("in_hi_ready")
        s_dt, s_dtu, s_zero = sem("dt_ready"), sem("dtu_ready"), sem("zero_ready")
        s_bps, s_cps, s_ball = sem("b_full"), sem("c_full"), sem("b_copied")
        s_dA, s_inflow, s_scan, s_read, s_acc = (sem("decay_ready"), sem("inflow_ready"), sem("scan_done"),
                                                 sem("read_ready"), sem("acc_done"))
        s_gtok, s_gt, s_gated = sem("gated_tok_ready"), sem("gated_transposed"), sem("gated_ready")
        s_mix, s_x1 = sem("mix_full"), sem("x1_ready")

        s_full = [sem("work_full0"), sem("work_full1")]
        s_evac = [sem("work_evac0"), sem("work_evac1")]
        s_stat, s_mv, s_vv, s_root, s_den, s_scale, s_ntok, s_nhi = (
            {m: sem("%s%d_s" % (n, m)) for m in NORMS}
            for n in ("stat", "mv", "vv", "root", "den", "scale", "n_tok", "n_hi"))
        s_sq, s_sqsum, s_rms, s_rden, s_rscale = (
            {c: sem("%s_%s_s" % (n, c)) for c in "ac"}
            for n in ("square", "sum", "rms", "rden", "rscale"))
        s_n1, s_n1lo = sem("norm1_full"), sem("norm1_out")
        s_inlo, s_keep, s_gate1, s_hid, s_mixed, s_x2b = (sem("in_lo_ready"), sem("keep_ready"), sem("gate1_ready"),
                                                          sem("hid_ready"), sem("mixed_ready"), sem("x2b_ready"))

        def wait(eng, s, value):
            if not (isinstance(value, int) and value == 0):
                eng.wait_ge(s, value)

        def full(eng, i, p):
            wait(eng, s_full[WORK_BANK[p]], mark(i, p))

        def evacuated(eng, i, p):
            wait(eng, s_evac[WORK_BANK[p]], mark(i, p))

        def bank_free(eng, i, p):
            wait(eng, s_evac[WORK_BANK[p]], mark(i, p) - 1)

        def work_of(p):
            return work[WORK_BANK[p]]

        def made(p):
            return s_full[WORK_BANK[p]], 1

        def emptied(p):
            return s_evac[WORK_BANK[p]], 1

        def cols(j):
            return slice(j * P, (j + 1) * P)

        def rounds(eng, pre, mix, a, b, c, extra, late=None):
            def one(i, parts):
                for s in range(SLOTS):
                    if "p" in parts:
                        pre(i + 1, s)
                    if "m" in parts:
                        mix(i, s)
                    if "a" in parts:
                        a(i, i - 1, s)
                    if "c" in parts:
                        c(i, i - 3, s)
                    if "b" in parts:
                        b(i, i - 2, s)
                    if late is not None and "m" in parts:
                        late(i, s)
                    if extra is not None and isinstance(i, int) and i >= 0:
                        extra(i, s)
            one(-1, "p")
            one(0, "pm")
            one(1, "pma")
            one(2, "pmab")
            with eng.Fori(FIRST_FULL, ROWS - 1) as i:
                one(i, "pmabc")
            one(ROWS - 1, "mabc")
            one(ROWS, "abc")
            one(ROWS + 1, "bc")
            one(ROWS + 2, "c")

        block = ctx.enter_context(nc.Block())

        W_MIX, W_TAIL = 16 * (9 + 2 + 4), 16 * (9 + TILES)

        @block.sync
        def _(sp):
            def load_x(b):
                wait(sp, s_htok, b)
                wait(sp, s_base, b)
                sp.dma_start(x_tok[:, :, :], x[bass.ds(b, 1), :, :].rearrange("a (j p) d -> (a p) j d", p=P)
                             ).then_inc(s_x_in, 16)

            def store(i, t):
                evacuated(sp, i, "c.down")
                sp.dma_start(out[bass.ds(t, 1), :, :].rearrange("a (j p) d -> (a p) j d", p=P), out_tok[:, :, :]
                             ).then_inc(s_out, 16)

            load_x(0)
            sp.sem_inc(s_out, 16)
            for dst, src in ((gamma_c[:, :], gamma.rearrange("(p a) -> p a", a=1)),
                             (beta_c[:, :], beta.rearrange("(p a) -> p a", a=1)),
                             (win_f, W_in),
                             (taps_c[:, :, :], W_conv.rearrange("(h p) k -> p h k", p=P)),
                             (b_conv_c[:, :], b_conv.rearrange("(h p) -> p h", p=P)),
                             (b_dt_c[:, :], b_dt.rearrange("(h p) -> p h", p=P)),
                             (decay_c[:, :, :], A_log.rearrange("(h p) n -> p h n", p=P)),
                             (skip_c[:, :], Dskip.rearrange("(h p) -> p h", p=P)),
                             (wout_sb[:, :, :], W_out.rearrange("(h p) n -> p h n", p=P))):
                sp.dma_start(dst, src, allow_slow_non_contiguous=True).then_inc(s_w_mix, 16)
            sp.wait_ge(s_wxz, 2)
            wx = W_x.rearrange("(h p) r -> p h r", p=P)
            for at in (0, 2 * STATE):
                sp.dma_start(wx_rep[:, :, at:at + 2 * STATE], wx[:, :, RANK:RANK + 2 * STATE]).then_inc(s_w_mix, 16)
            for at in (64, 96):
                sp.dma_start(wx_rep[:, :, at:at + RANK], wx[:, :, 0:RANK]).then_inc(s_w_mix, 16)
                sp.dma_start(wdt_f[at:at + RANK, :], W_dt).then_inc(s_w_mix, 16)
            for dst, src in ((up_raw[:, :, :], w_up.rearrange("(k p) d -> p k d", p=P)),
                             (down_raw, w_down),
                             (w12_f[:, 0:FF], W1), (w12_f[:, FF:2 * FF], W2),
                             (b1_c[:, :], b1.rearrange("(k p) -> p k", p=P)),
                             (b2_c[:, :], b2.rearrange("(k p) -> p k", p=P)),
                             (bz_c[:, :], bz.rearrange("(k p) -> p k", p=P)),
                             (bh_c[:, :], bh.rearrange("(k p) -> p k", p=P)),
                             (wo_sb[:, :, :], Wo.rearrange("(k p) n -> p k n", p=P))):
                sp.dma_start(dst, src, allow_slow_non_contiguous=True).then_inc(s_w_tail, 16)
            for j in range(TILES):
                sp.dma_start(bo_tok[:, j, :], bo.partition_broadcast(P)).then_inc(s_w_tail, 16)
            sp.dma_start(wzh_f[:, :, 0:FF], Wz.rearrange("(k p) n -> p k n", p=P)).then_inc(s_w_zh, 16)
            sp.dma_start(wzh_f[:, :, FF:2 * FF], Wh.rearrange("(k p) n -> p k n", p=P)).then_inc(s_w_zh, 16)

            for i in range(1, FIRST_FULL + 1):
                load_x(i)
            with sp.Fori(FIRST_FULL, ROWS - 1) as i:
                load_x(i + 1)
                store(i, i - 3)
            for i in range(ROWS - 1, ROUNDS):
                store(i, i - 3)
            sp.wait_ge(s_out, 16 * ROWS + 16)

        @block.gpsimd
        def _(pool):
            pool.memset(wx_rep[:, :, :], 0.0).then_inc(s_wxz, 1)
            pool.memset(wdt_f[:, :], 0.0).then_inc(s_wxz, 1)
            pool.memset(ones[:, :], 1.0).then_inc(s_const, 1)
            pool.memset(minus_half[:, :], -0.5).then_inc(s_const, 1)
            pool.memset(plus_half[:, :], 0.5).then_inc(s_const, 1)
            pool.memset(ident[:, :], 0.0).then_inc(s_eye, 1)
            pool.wait_ge(s_eye, 1)
            pool.affine_select(out=ident[:, :], in_=ident[:, :], compare_op=ALU.not_equal, fill=1.0,
                               base=0, pattern=[[-1, P]], channel_multiplier=1).then_inc(s_eye, 1)

            def prepare(i, s):
                if (i, s) == (0, SCAN + 2):
                    pool.wait_ge(s_w_tail, W_TAIL)
                    pool.wait_ge(s_hi12, 1)
                    pool.tensor_tensor(w12_lo[:, :], w12_f, w12_hi[:, :].bitcast(F32), ALU.subtract
                                       ).then_inc(s_lo12, 1)
                    pool.tensor_scalar(bzh_c[:, :], bz_c[:, :], 0.5, None, ALU.mult).then_inc(s_bzh, 1)
                if i == 0 and s in (SCAN + 4, SCAN + 6, SCAN + 8, SCAN + 10):
                    k = (s - SCAN - 4) // 2
                    pool.wait_ge(s_hizh, k + 1)
                    pool.tensor_tensor(wzh_lo[:, k, :], wzh_f[:, k, :], wzh_hi[:, k, :].bitcast(F32), ALU.subtract
                                       ).then_inc(s_lozh, 1)

            def mix_root(b):
                pool.wait_ge(s_mvv, b + 1)
                pool.tensor_tensor(flat(m_root[:, :, :]), flat(m_vv[:, :, :]), minus_half[:, :], ALU.pow
                                   ).then_inc(s_mroot, 1)

            def mix_base(b):
                pool.wait_ge(s_mgs, 2 * b + 2)
                wait(pool, s_x1, b)
                pool.sem_inc(s_passed)
                for j in range(TILES):
                    last = pool.tensor_scalar(base_tok[:, j, :], x_tok[:, j, :], m_gain[:, j:j + 1],
                                              m_shift[:, j:j + 1], ALU.mult, ALU.add)
                last.then_inc(s_base, 1)

            def mix_h_lo(b):
                pool.wait_ge(s_hhi, b + 1)
                wait(pool, s_z, 2 * b)
                pool.tensor_tensor(h_lo[:, :], h_f, h_hi[:, :].bitcast(F32), ALU.subtract).then_inc(s_hlo, 1)

            def mix_inflow(b, n):
                pool.wait_ge(s_ball, STATE * b + n + 1)
                pool.wait_ge(s_scan, STATE * b + n - 1)
                pool.tensor_tensor(inflow[:, n % 2, :, :], dtu[:, :, :],
                                   b_all[:, n % 2, :].unsqueeze(1).broadcast_to([P, HALVES, SEQ]), ALU.mult
                                   ).then_inc(s_inflow, 1)

            def pre(b, s):
                if s == 3:
                    mix_root(b)
                if s == 19:
                    mix_h_lo(b)

            def mix(b, s):
                n = s - SCAN
                if s == 1:
                    mix_base(b)
                if 1 <= n < STATE - 1:
                    mix_inflow(b, n + 1)

            def norm_root(t, m):
                pool.wait_ge(s_vv[m], t + 1)
                pool.tensor_tensor(flat(root[m][:, :, :]), flat(vv[m][:, :, :]),
                                   (minus_half if m == 2 else plus_half)[:, :], ALU.pow).then_inc(s_root[m], 1)

            def ffn_sumsq(t, c, k):
                sq = square[c]
                pool.wait_ge(s_sq[c], FB * t + k + 1)
                if k > 1:
                    pool.wait_ge(s_sqsum[c], 3 * t + k - 1)
                pool.tensor_tensor(sq_sum[c], sq[:, 0, :], sq[:, k, :], ALU.add).then_inc(s_sqsum[c], 1)

            def ffn_rms(i, c):
                evacuated(pool, i, c + ".sumsq")
                pool.tensor_tensor(rms[c][:, :], ms[c][:, :], plus_half[:, 0:TILES], ALU.pow).then_inc(s_rms[c], 1)

            def gru_in_lo(t, j):
                pool.wait_ge(s_inhi, FB * t + j + 1)
                pool.tensor_tensor(in_lo[:, j, :], in_f[:, j, :], in_hi[:, j, :].bitcast(F32), ALU.subtract
                                   ).then_inc(s_inlo, 1)

            def gru_keep(t, j):
                pool.wait_ge(s_gate1, FB * t + j + 1)
                if j >= 2:
                    pool.wait_ge(s_hid, FB * t + j - 1)
                pool.sem_inc(s_passed)
                pool.tensor_scalar(keep[:, j % 2, :], gate[:, j % 2, :], -0.5, 1.0, ALU.mult, ALU.add
                                   ).then_inc(s_keep, 1)

            def x2b(i, t):
                evacuated(pool, i, "a.down")
                if not isinstance(i, int) or i >= LAG["b"]:
                    evacuated(pool, i, "b.out")
                pool.tensor_tensor(x2b_tok[:, :, :], x2_tok[:, :, :], bo_tok[:, :, :], ALU.add).then_inc(s_x2b, 1)

            def a(i, t, s):
                if s == 0:
                    norm_root(t, 1)
                if s in (11, 12, 13):
                    ffn_sumsq(t, "a", s - 10)
                if s == 15:
                    ffn_rms(i, "a")
                if s == 17:
                    norm_root(t, 2)
                if s == 19:
                    x2b(i, t)
                if s == 23:
                    gru_in_lo(t, 0)
                    gru_in_lo(t, 1)

            def b(i, t, s):
                if s == 0:
                    gru_in_lo(t, 2)
                    gru_in_lo(t, 3)
                if s in KEEP_SLOTS:
                    gru_keep(t, KEEP_SLOTS.index(s))
                if s == 15:
                    norm_root(t, 3)

            def c(i, t, s):
                if s in (5, 7, 8):
                    ffn_sumsq(t, "c", (5, 7, 8).index(s) + 1)
                if s == 10:
                    ffn_rms(i, "c")

            pool.wait_ge(s_const, 3)
            rounds(pool, pre, mix, a, b, c, prepare)

        @block.scalar
        def _(act):
            def prepare(i, s):
                if (i, s) == (0, SCAN + 1):
                    act.wait_ge(s_w_tail, W_TAIL)
                    act.activation(w12_hi[:, :], w12_f, ACT.Copy).then_inc(s_hi12, 1)
                    act.wait_ge(s_w_zh, 32)
                if i == 0 and s in (SCAN + 3, SCAN + 5, SCAN + 7, SCAN + 9):
                    k = (s - SCAN - 3) // 2
                    act.activation(wzh_hi[:, k, :], wzh_f[:, k, :], ACT.Copy).then_inc(s_hizh, 1)
                if (i, s) == (0, SCAN + 11):
                    act.wait_ge(s_tern_t, 1)
                    act.activation(up_t[:, :], work[0][:, :], ACT.Copy).then_inc(s_tern, 1)
                    act.wait_ge(s_tern_t, 2)
                    act.activation(flat(down_t[:, :, :]), work[1][:, :], ACT.Copy).then_inc(s_tern, 1)

            def mix_h(b):
                act.wait_ge(s_ht, b + 1)
                act.activation(h_f, b_ps[:, :], ACT.Identity, bias=beta_c[:, 0:1], scale=gamma_c[:, 0:1])
                act.activation(h_hi[:, :], b_ps[:, :], ACT.Identity, bias=beta_c[:, 0:1], scale=gamma_c[:, 0:1]
                               ).then_inc(s_hhi, 1)

            def mix_z(b, i):
                act.wait_ge(s_z, 2 * b + 2 - i)
                act.activation(flat(z_tok[:, 2 * i:2 * i + 2, :]), y_ps[i][:, :], ACT.Silu).then_inc(s_ztok, 1)

            def mix_u(b, h):
                act.wait_ge(s_conv, HALVES * TAPS * b + TAPS * (h + 1))
                act.activation(u[:, h, :], conv[:, h, :], ACT.Silu).then_inc(s_u, 1)

            def mix_xd(b):
                act.wait_ge(s_xdbl, b + 1)
                act.activation(xd[:, :], b_ps[:, :], ACT.Copy).then_inc(s_xdhi, 1)

            def mix_softplus(b):
                act.preload_act_table_set("natural_log_exp_and_others")
                for h in range(HALVES):
                    act.wait_ge(s_relu, HALVES * b + h + 1)
                    act.activation(sp_abs[:, h, :], dA[:, h, :], ACT.Abs, bias=b_dt_c[:, h:h + 1]
                                   ).then_inc(s_sparg, 1)
                act.wait_ge(s_sparg, HALVES * b + HALVES)
                act.activation(sp_abs, sp_abs, ACT.Exp, scale=-1.0).then_inc(s_spexp, 1)
                act.wait_ge(s_spexp, b + 1)
                act.activation(sp_abs, sp_abs, ACT.Ln, bias=1.0).then_inc(s_spln, 1)

            def mix_b(b, n):
                act.wait_ge(s_bps, STATE * b + n + 1)
                act.wait_ge(s_inflow, STATE * b + n - 1)
                act.activation(b_all[:, n % 2, :], b_ps[:, :], ACT.Copy).then_inc(s_ball, 1)

            def mix_decay(b, n):
                if n == 0:
                    act.wait_ge(s_dt, b + 1)
                    act.wait_ge(s_zero, b + 1)
                else:
                    act.wait_ge(s_scan, STATE * b + n)
                act.activation(dA[:, 0, :], dt[:, 0, :], ACT.Exp, scale=decay_c[:, 0, n:n + 1])
                act.activation(dA[:, 1, 1:SEQ], dt[:, 1, 1:SEQ], ACT.Exp, scale=decay_c[:, 1, n:n + 1]
                               ).then_inc(s_dA, 1)

            def mix_gated(b, h):
                act.wait_ge(s_gt, HALVES * b + h + 1)
                act.activation(gated[:, h, :], (b_ps, c_ps)[h][:, :], ACT.Copy).then_inc(s_gated, 1)

            def pre(b, s):
                if s == 19:
                    mix_h(b)
                if s == BACK + 2:
                    mix_u(b, 0)
                    mix_u(b, 1)
                if s == BACK + 3:
                    mix_xd(b)

            def mix(b, s):
                n = s - SCAN
                if s == 0:
                    mix_z(b, 1)
                    mix_z(b, 0)
                if s == 1:
                    mix_softplus(b)
                if s == 2:
                    mix_decay(b, 0)
                if 0 <= n < STATE - 1:
                    mix_decay(b, n + 1)
                if 0 <= n < STATE - 2:
                    mix_b(b, n + 2)
                if s == BACK + 1:
                    mix_gated(b, 0)
                    mix_gated(b, 1)

            def norm_hi(i, m):
                if m == 1:
                    act.wait_ge(s_n1, i)
                    src = c_ps
                else:
                    p = {2: "a.norm2", 3: "b.norm3"}[m]
                    full(act, i, p)
                    src = work_of(p)
                act.activation(n_hi[m][:, :], src[:, :], ACT.Copy).then_inc(s_nhi[m], 1)

            def ffn_gelu(i, c, j):
                p = c + ".up%d" % j
                full(act, i, p)
                act.activation(gelu[c][:, j, :], work_of(p)[:, :], ACT.Gelu).then_inc(*emptied(p))

            def ffn_square(i, c, j):
                evacuated(act, i, c + ".up%d" % j)
                act.activation(square[c][:, j, :], gelu[c][:, j, :], ACT.Square).then_inc(s_sq[c], 1)

            def gru_in(i, j):
                p = ("a.in%d" if j < 6 else "b.in%d") % j
                full(act, i, p)
                if j < FB:
                    act.activation(in_f[:, j, :], work_of(p)[:, :], ACT.Silu, bias=b1_c[:, j:j + 1]
                                   ).then_inc(*emptied(p))
                else:
                    act.activation(skip_f[:, j - FB, :], work_of(p)[:, :], ACT.Silu, bias=b2_c[:, j - FB:j - FB + 1]
                                   ).then_inc(*emptied(p))

            def gru_gate(i, t, j):
                p = "b.z%d" % j
                full(act, i, p)
                if j >= 2:
                    evacuated(act, i, "b.h%d" % (j - 2))
                    act.wait_ge(s_keep, FB * t + j - 1)
                act.activation(gate[:, j % 2, :], work_of(p)[:, :], ACT.Tanh, scale=0.5, bias=bzh_c[:, j:j + 1]
                               ).then_inc(*emptied(p))
                evacuated(act, i, p)
                act.activation(gate[:, j % 2, :], gate[:, j % 2, :], ACT.Copy, bias=1.0).then_inc(s_gate1, 1)

            IN_AT = {22: (0, 1), 23: (2, 3, 4, 5)}

            def a(i, t, s):
                if s == 1:
                    norm_hi(i, 1)
                if s == 3:
                    for j in range(FB):
                        ffn_gelu(i, "a", j)
                if s in (8, 10):
                    ffn_square(i, "a", s - 8)
                    ffn_square(i, "a", s - 7)
                if s == 19:
                    norm_hi(i, 2)
                for j in IN_AT.get(s, ()):
                    gru_in(i, j)

            def b(i, t, s):
                if s == 0:
                    gru_in(i, 6)
                    gru_in(i, 7)
                if s in GATE_SLOTS:
                    gru_gate(i, t, GATE_SLOTS.index(s))
                if s == 17:
                    norm_hi(i, 3)

            def c(i, t, s):
                if s == 2:
                    for j in range(FB):
                        ffn_gelu(i, "c", j)
                if s in (4, 6):
                    ffn_square(i, "c", s - 4)
                    ffn_square(i, "c", s - 3)

            act.wait_ge(s_w_mix, W_MIX)
            act.activation(decay_c[:, :, :], decay_c[:, :, :], ACT.Exp).then_inc(s_expA, 1)
            rounds(act, pre, mix, a, b, c, prepare)

        @block.vector
        def _(dve):
            def prepare_mix():
                dve.wait_ge(s_eye, 2)
                dve.tensor_tensor(pick[:, :], ident[:, 0:2 * STATE], ident[:, 2 * STATE:4 * STATE], ALU.add
                                  ).then_inc(s_pick, 1)
                dve.wait_ge(s_w_mix, W_MIX)
                dve.tensor_copy(win_hi[:, :], win_f).then_inc(s_win_hi, 1)
                dve.tensor_copy(wdt_hi[:, :], wdt_f[:, :]).then_inc(s_wdt_hi, 1)
                dve.wait_ge(s_win_hi, 1)
                dve.tensor_tensor(win_lo[:, :], win_f, win_hi[:, :].bitcast(F32), ALU.subtract).then_inc(s_win, 1)
                dve.wait_ge(s_wdt_hi, 1)
                dve.tensor_tensor(wdt_lo[:, :], wdt_f[:, :], wdt_hi[:, :].bitcast(F32), ALU.subtract
                                  ).then_inc(s_wdt, 1)
                dve.wait_ge(s_expA, 1)
                dve.tensor_scalar(decay_c[:, :, :], decay_c[:, :, :], -1.0, None, ALU.mult).then_inc(s_A, 1)

            def prepare(i, s):
                if (i, s) == (0, SCAN + 2):
                    dve.wait_ge(s_w_tail, W_TAIL)
                    dve.tensor_reduce(abs_sum[:, 0:1], flat(up_raw[:, :, :]), AX_X, ALU.add,
                                      apply_absolute_value=True).then_inc(s_abs, 1)
                    dve.tensor_reduce(abs_sum[:, 1:2], down_raw, AX_X, ALU.add, apply_absolute_value=True
                                      ).then_inc(s_abs, 1)
                if (i, s) == (0, SCAN + 4):
                    dve.wait_ge(s_abs_all, 1)
                    dve.tensor_scalar(thr[:, :], work[0][:, 0:2], 0.5 / (FF * D), None, ALU.mult).then_inc(s_thr, 1)
                    dve.tensor_scalar(thr_neg[:, :], work[0][:, 0:2], -0.5 / (FF * D), None, ALU.mult
                                      ).then_inc(s_thr, 1)
                    dve.wait_ge(s_thr, 2)
                if (i, s) in ((0, SCAN + 5), (0, SCAN + 7)):
                    k = (s - SCAN - 5) // 2
                    raw, sign = ((flat(up_raw[:, :, :]), flat(up_sign[:, :, :])), (down_raw, down_sign))[k]
                    dve.tensor_scalar(below, raw, thr_neg[:, k:k + 1], None, ALU.is_lt).then_inc(s_below, 1)
                    dve.wait_ge(s_below, k + 1)
                    dve.scalar_tensor_tensor(sign, raw, thr[:, k:k + 1], below, ALU.is_gt, ALU.subtract
                                             ).then_inc(s_sign, 1)
                    dve.wait_ge(s_sign, k + 1)

            def mix_norm(b):
                dve.wait_ge(s_x_in, 16 * b + 16)
                for j in range(TILES):
                    last = dve.bn_stats(m_stat[:, j, :], x_tok[:, j, :])
                last.then_inc(s_mstat, 1)
                dve.wait_ge(s_mstat, b + 1)
                dve.sem_inc(s_passed)
                for j in range(TILES):
                    last = dve.bn_aggr(m_mv[:, j, :], m_stat[:, j, :])
                last.then_inc(s_mmv, 1)
                dve.wait_ge(s_mmv, b + 1)
                dve.tensor_scalar(m_vv[:, 0, :], m_mv[:, :, 1], LN_EPS, None, ALU.add)
                dve.tensor_scalar(m_vv[:, 1, :], m_mv[:, :, 1], 1.0 + LN_EPS, LN_EPS * LN_EPS, ALU.mult, ALU.add
                                  ).then_inc(s_mvv, 1)

            def mix_apply(b):
                dve.wait_ge(s_mroot, b + 1)
                wait(dve, s_base, b)
                dve.tensor_scalar(m_gain[:, :], m_root[:, 0, :], 1.0, None, ALU.add).then_inc(s_mgs, 1)
                dve.scalar_tensor_tensor(m_shift[:, :], m_mv[:, :, 0], -1.0, m_root[:, 0, :], ALU.mult, ALU.mult
                                         ).then_inc(s_mgs, 1)
                wait(dve, s_hlo, b)
                for j in range(TILES):
                    last = dve.tensor_scalar(h_tok[:, j, :], x_tok[:, j, :], m_mv[:, j, 0:1], m_root[:, 1, j:j + 1],
                                             ALU.subtract, ALU.mult)
                last.then_inc(s_htok, 1)

            def mix_conv(b, h):
                if not (isinstance(b, int) and b == 0):
                    dve.wait_ge(s_acc, STATE * b - 1)
                for s in range(TAPS):
                    w = taps_c[:, h, TAPS - 1 - s:TAPS - s]
                    if s == 0:
                        dve.wait_ge(s_xi, HALVES * b + h + 1)
                        dve.tensor_scalar(conv[:, h, :], dA[:, h, :], w, b_conv_c[:, h:h + 1], ALU.mult, ALU.add
                                          ).then_inc(s_conv, 1)
                    else:
                        dve.wait_ge(s_conv, HALVES * TAPS * b + TAPS * h + s)
                        dve.scalar_tensor_tensor(conv[:, h, s:SEQ], dA[:, h, 0:SEQ - s], w, conv[:, h, s:SEQ],
                                                 ALU.mult, ALU.add).then_inc(s_conv, 1)

            def mix_skip(b):
                dve.wait_ge(s_u, HALVES * b + HALVES)
                for h in range(HALVES):
                    last = dve.tensor_scalar(skip_u[:, h, :], u[:, h, :], skip_c[:, h:h + 1], None, ALU.mult)
                last.then_inc(s_skip, 1)

            def mix_xd_lo(b):
                dve.wait_ge(s_xdhi, b + 1)
                for q in (32, 96):
                    last = dve.tensor_tensor(xd[q:q + 32, :], b_ps[q:q + 32, :], xd[q:q + 32, :].bitcast(F32),
                                             ALU.subtract)
                last.then_inc(s_xdlo, 1)

            def mix_relu(b, h):
                dve.wait_ge(s_dtp, HALVES * b + h + 1)
                dve.tensor_scalar(sp_relu[:, h, :], dA[:, h, :], b_dt_c[:, h:h + 1], 0.0, ALU.add, ALU.max
                                  ).then_inc(s_relu, 1)

            def mix_b(b, n):
                dve.wait_ge(s_bps, STATE * b + n + 1)
                dve.tensor_copy(b_all[:, n, :], b_ps[:, :]).then_inc(s_ball, 1)

            def mix_zero(b):
                dve.wait_ge(s_sparg, HALVES * b + HALVES)
                dve.tensor_scalar(dA[:, 1, 0:1], ones[:, 0:1], 0.0, None, ALU.mult).then_inc(s_zero, 1)

            def mix_dt(b):
                dve.wait_ge(s_spln, b + 1)
                wait(dve, s_dA, STATE * b)
                dve.tensor_tensor(dt[:, :, :], sp_relu[:, :, :], sp_abs, ALU.add).then_inc(s_dt, 1)
                dve.wait_ge(s_dt, b + 1)
                dve.tensor_tensor(dtu[:, :, :], dt[:, :, :], u[:, :, :], ALU.mult).then_inc(s_dtu, 1)

            def mix_inflow(b, n):
                dve.wait_ge(s_dtu, b + 1)
                dve.wait_ge(s_ball, STATE * b + n + 1)
                if n == 0:
                    wait(dve, s_mix, b)
                else:
                    dve.wait_ge(s_y0, b + 1)
                dve.tensor_tensor(inflow[:, n, :, :], dtu[:, :, :],
                                  b_all[:, n, :].unsqueeze(1).broadcast_to([P, HALVES, SEQ]), ALU.mult
                                  ).then_inc(s_inflow, 1)

            def mix_scan(b, n):
                dve.wait_ge(s_dA, STATE * b + n + 1)
                dve.wait_ge(s_inflow, STATE * b + n + 1)
                if n >= 3:
                    dve.wait_ge(s_acc, STATE * b + n - 2)
                dve.tensor_tensor_scan(flat(state[:, n % 3, :, :]), flat(dA[:, :, :]), flat(inflow[:, n % 2, :, :]),
                                       0.0, ALU.mult, ALU.add).then_inc(s_scan, 1)

            def mix_read(b, n):
                dve.wait_ge(s_scan, STATE * b + n + 1)
                dve.wait_ge(s_cps, STATE * b + n + 1)
                dve.tensor_tensor(state[:, n % 3, :, :], state[:, n % 3, :, :],
                                  c_ps[:, :].unsqueeze(1).broadcast_to([P, HALVES, SEQ]), ALU.mult
                                  ).then_inc(s_read, 1)

            def mix_gate(b):
                dve.wait_ge(s_acc, STATE * b + STATE)
                dve.wait_ge(s_ztok, 2 * b + 2)
                for i in range(2):
                    at = flat(z_tok[:, 2 * i:2 * i + 2, :])
                    dve.tensor_tensor(at, y_ps[i][:, :], at, ALU.mult).then_inc(s_gtok, 1)

            def mix_x1(b):
                dve.wait_ge(s_mix, b + 1)
                dve.wait_ge(s_base, b + 1)
                dve.tensor_tensor(flat(x1_tok[:, :, :]), y_ps[0][:, :], flat(base_tok[:, :, :]), ALU.add
                                  ).then_inc(s_x1, 1)

            def pre(b, s):
                if s == 3:
                    mix_norm(b)
                    mix_apply(b)
                if s == BACK + 1:
                    mix_conv(b, 0)
                    if not (isinstance(b, int) and b == 0):
                        mix_gate(b - 1)
                    mix_conv(b, 1)
                if s == BACK + 3:
                    mix_xd_lo(b)

            def mix(b, s):
                n = s - SCAN
                if s == 1:
                    mix_b(b, 0)
                if s == 2:
                    mix_zero(b)
                    mix_dt(b)
                    mix_inflow(b, 0)
                    mix_b(b, 1)
                    mix_inflow(b, 1)
                if 0 <= n < STATE:
                    mix_scan(b, n)
                if 1 <= n <= STATE:
                    mix_read(b, n - 1)
                if s == BACK + 1 and isinstance(b, int) and b == ROWS - 1:
                    mix_gate(b)
                if s == BACK + 3:
                    mix_x1(b)

            def late(b, s):
                if s == 0:
                    mix_relu(b, 0)
                    mix_relu(b, 1)
                    mix_skip(b)

            def norm_stats(t, m, src):
                for j in range(TILES):
                    last = dve.bn_stats(stat[m][:, j, :], src[:, j, :])
                last.then_inc(s_stat[m], 1)
                dve.wait_ge(s_stat[m], t + 1)
                dve.sem_inc(s_passed)
                for j in range(TILES):
                    last = dve.bn_aggr(mv[m][:, j, :], stat[m][:, j, :])
                last.then_inc(s_mv[m], 1)
                dve.wait_ge(s_mv[m], t + 1)
                for k, eps in enumerate((LN_EPS, LN_EPS) if m == 2 else (0.0, LN_EPS)):
                    last = dve.tensor_scalar(vv[m][:, k, :], mv[m][:, :, 1], eps, None, ALU.add)
                last.then_inc(s_vv[m], 1)

            def norm_apply(t, m, src):
                dve.wait_ge(s_root[m], t + 1)
                by = root[m][:, 0, :]
                if m != 2:
                    dve.scalar_tensor_tensor(den[m][:, :], root[m][:, 1, :], RMS_EPS, root[m][:, 0, :],
                                             ALU.mult, ALU.add).then_inc(s_den[m], 1)
                    dve.wait_ge(s_den[m], t + 1)
                    dve.reciprocal(scale[m][:, :], den[m][:, :]).then_inc(s_scale[m], 1)
                    dve.wait_ge(s_scale[m], t + 1)
                    by = scale[m]
                for j in range(TILES):
                    last = dve.tensor_scalar(n_tok[:, j, :], src[:, j, :], mv[m][:, j, 0:1], by[:, j:j + 1],
                                             ALU.subtract, ALU.mult)
                last.then_inc(s_ntok[m], 1)

            def norm_lo(i, t, m):
                dve.wait_ge(s_nhi[m], t + 1)
                if m == 1:
                    dve.tensor_tensor(n_lo[1][:, :], c_ps[:, :], n_hi[1][:, :].bitcast(F32), ALU.subtract
                                      ).then_inc(s_n1lo, 1)
                else:
                    p = {2: "a.norm2", 3: "b.norm3"}[m]
                    dve.tensor_tensor(n_lo[m][:, :], work_of(p)[:, :], n_hi[m][:, :].bitcast(F32), ALU.subtract
                                      ).then_inc(*emptied(p))

            def ffn_ms(i, c):
                p = c + ".sumsq"
                full(dve, i, p)
                dve.tensor_scalar(ms[c][:, :], work_of(p)[:, 0:TILES], 1.0 / FF, None, ALU.mult
                                  ).then_inc(*emptied(p))

            def ffn_out(i, t, c, src, dst):
                p = c + ".down"
                dve.wait_ge(s_rms[c], t + 1)
                dve.tensor_scalar(rden[c][:, :], rms[c][:, :], RMS_EPS, None, ALU.add).then_inc(s_rden[c], 1)
                dve.wait_ge(s_rden[c], t + 1)
                dve.reciprocal(rscale[c][:, :], rden[c][:, :]).then_inc(s_rscale[c], 1)
                dve.wait_ge(s_rscale[c], t + 1)
                full(dve, i, p)
                for j in range(TILES):
                    last = dve.scalar_tensor_tensor(dst[:, j, :], work_of(p)[:, cols(j)], rscale[c][:, j:j + 1],
                                                    src[:, j, :], ALU.mult, ALU.add)
                last.then_inc(*emptied(p))

            def gru_in_hi(i, t, j):
                evacuated(dve, i, "a.in%d" % j)
                dve.tensor_copy(in_hi[:, j, :], in_f[:, j, :]).then_inc(s_inhi, 1)

            def gru_new(i, t, j):
                p = "b.h%d" % j
                full(dve, i, p)
                dve.wait_ge(s_gate1, FB * t + j + 1)
                dve.scalar_tensor_tensor(mixed[:, j, :], work_of(p)[:, :], bh_c[:, j:j + 1], gate[:, j % 2, :],
                                         ALU.add, ALU.mult).then_inc(*emptied(p))

            def gru_scan(i, t, j):
                evacuated(dve, i, "b.h%d" % j)
                dve.wait_ge(s_keep, FB * t + j + 1)
                dve.tensor_tensor_scan(mixed[:, j, :], keep[:, j % 2, :], mixed[:, j, :], 0.0,
                                       ALU.mult, ALU.add).then_inc(s_hid, 1)

            def gru_mixed(t, j):
                dve.wait_ge(s_hid, FB * t + j + 1)
                dve.scalar_tensor_tensor(mixed[:, j, :], mixed[:, j, :], 0.5, skip_f[:, j, :], ALU.mult, ALU.add
                                         ).then_inc(s_mixed, 1)

            def gru_out(i, t):
                full(dve, i, "b.out")
                dve.wait_ge(s_x2b, t + 1)
                dve.wait_ge(s_out, 16 * t + 16)
                dve.tensor_tensor(flat(x3_tok[:, :, :]), work_of("b.out")[:, :], flat(x2b_tok[:, :, :]), ALU.add
                                  ).then_inc(*emptied("b.out"))

            def a(i, t, s):
                if s == 0:
                    dve.wait_ge(s_x1, t + 1)
                    norm_stats(t, 1, x1_tok)
                if s == 1:
                    norm_apply(t, 1, x1_tok)
                if s == 2:
                    norm_lo(i, t, 1)
                if s == 14:
                    ffn_ms(i, "a")
                if s == 17:
                    ffn_out(i, t, "a", x1_tok, x2_tok)
                    evacuated(dve, i, "a.down")
                    norm_stats(t, 2, x2_tok)
                if s == 18:
                    if not isinstance(i, int) or i >= LAG["b"]:
                        full(dve, i, "b.norm3")
                    norm_apply(t, 2, x2_tok)
                if s == 19:
                    norm_lo(i, t, 2)
                if s == 23:
                    for j in range(FB):
                        gru_in_hi(i, t, j)

            def b(i, t, s):
                if s in NEW_SLOTS:
                    j = NEW_SLOTS.index(s)
                    gru_new(i, t, j)
                if s in HID_SLOTS:
                    j = HID_SLOTS.index(s)
                    gru_scan(i, t, j)
                    gru_mixed(t, j)
                if s == 15:
                    gru_out(i, t)
                    evacuated(dve, i, "b.out")
                    norm_stats(t, 3, x3_tok)
                if s == 16:
                    norm_apply(t, 3, x3_tok)
                if s == 18:
                    norm_lo(i, t, 3)

            def c(i, t, s):
                if s == 9:
                    ffn_ms(i, "c")
                if s == 13:
                    ffn_out(i, t, "c", x3_tok, out_tok)

            dve.wait_ge(s_const, 3)
            prepare_mix()
            rounds(dve, pre, mix, a, b, c, prepare, late)

        @block.tensor
        def _(pe):
            def three(dst, w_hi, w_lo, r_hi, r_lo, start=True, stop=True):
                pe.matmul(dst, w_hi, r_hi, start=start, stop=False)
                pe.matmul(dst, w_lo, r_hi, start=False, stop=False)
                return pe.matmul(dst, w_hi, r_lo, start=False, stop=stop)

            def prepare(i, s):
                if (i, s) == (0, SCAN + 3):
                    pe.wait_ge(s_abs, 2)
                    pe.matmul(work[0][:, 0:2], ones[:, :], abs_sum[:, :], start=True, stop=True
                              ).then_inc(s_abs_all, 1)
                if (i, s) == (0, SCAN + 10):
                    pe.wait_ge(s_sign, 1)
                    for k in range(FB):
                        last = pe.transpose(work[0][:, cols(k)], up_sign[:, k, :], ident[:, :])
                    last.then_inc(s_tern_t, 1)
                    pe.wait_ge(s_sign, 2)
                    for k in range(FB):
                        last = pe.transpose(work[1][:, cols(k)], down_sign[:, cols(k)], ident[:, :])
                    last.then_inc(s_tern_t, 1)
                if (i, s) == (0, SLOTS - 1):
                    pe.wait_ge(s_tern, 2)
                    pe.wait_ge(s_lo12, 1)
                    pe.wait_ge(s_lozh, FB)

            def mix_ht(b):
                pe.wait_ge(s_htok, b + 1)
                wait(pe, s_ball, STATE * b)
                for j in range(TILES):
                    last = pe.transpose(b_ps[:, cols(j)], h_tok[:, j, :], ident[:, :])
                last.then_inc(s_ht, 1)

            def mix_in(b):
                pe.wait_ge(s_hhi, b + 1)
                pe.wait_ge(s_hlo, b + 1)
                wait(pe, s_scan, STATE * b)
                for h in range(HALVES):
                    three(dA[:, h, :], win_hi[:, cols(h)], win_lo[:, cols(h)], h_hi[:, :], h_lo[:, :]
                          ).then_inc(s_xi, 1)

            def mix_zin(b, i):
                if i == 1:
                    wait(pe, s_gtok, 2 * b)
                else:
                    wait(pe, s_x1, b)
                for j in (2 * i, 2 * i + 1):
                    at = slice((j % 2) * INNER, (j % 2 + 1) * INNER)
                    last = three(y_ps[i][:, at], h_hi[:, cols(j)], h_lo[:, cols(j)],
                                 win_hi[:, INNER:2 * INNER], win_lo[:, INNER:2 * INNER])
                last.then_inc(s_z, 1)

            def mix_xdbl(b):
                pe.wait_ge(s_u, HALVES * b + HALVES)
                wait(pe, s_gated, HALVES * b)
                for h in range(HALVES):
                    last = pe.matmul(b_ps[:, :], wx_rep[:, h, :], u[:, h, :], start=(h == 0), stop=(h == HALVES - 1))
                last.then_inc(s_xdbl, 1)

            def mix_dtp(b):
                pe.wait_ge(s_xdlo, b + 1)
                for h in range(HALVES):
                    pe.matmul(dA[:, h, :], wdt_hi[:, cols(h)], xd[:, :], start=True, stop=False)
                    pe.matmul(dA[:, h, :], wdt_lo[:, cols(h)], xd[:, :], start=False, stop=True).then_inc(s_dtp, 1)

            def y_region(j, h):
                at = (j % 2) * INNER + h * P
                return y_ps[j // 2][:, at:at + P]

            def mix_skip(b):
                pe.wait_ge(s_skip, b + 1)
                pe.wait_ge(s_ztok, 2 * b + 2)
                for j in range(TILES):
                    for h in range(HALVES):
                        last = pe.matmul(y_region(j, h), skip_u[:, h, cols(j)], ident[:, :], is_transpose=True,
                                         start=(j % 2 == 0 and h == 0), stop=False, skip_group_check=True)
                last.then_inc(s_y0, 1)

            def mix_bn(b, n):
                if n:
                    pe.wait_ge(s_ball, STATE * b + n)
                pe.matmul(b_ps[:, :], pick[:, n:n + 1].broadcast_to([P, P]), xd[:, :], start=True, stop=True).then_inc(s_bps, 1)

            def mix_cn(b, n):
                if n:
                    pe.wait_ge(s_read, STATE * b + n)
                pe.matmul(c_ps[:, :], pick[:, STATE + n:STATE + n + 1].broadcast_to([P, P]), xd[:, :], start=True, stop=True).then_inc(s_cps, 1)

            def mix_acc(b, n):
                pe.wait_ge(s_read, STATE * b + n + 1)
                for h in range(HALVES):
                    for j in range(TILES):
                        last = pe.matmul(y_region(j, h), state[:, n % 3, h, cols(j)], ident[:, :], is_transpose=True,
                                         start=False, stop=(n == STATE - 1), skip_group_check=True)
                last.then_inc(s_acc, 1)

            def mix_gt(b):
                pe.wait_ge(s_gtok, 2 * b + 2)
                if isinstance(b, int) and b == ROWS - 1:
                    pe.wait_ge(s_ball, STATE * b + STATE)
                else:
                    pe.wait_ge(s_hhi, b + 2)
                for h in range(HALVES):
                    for j in range(TILES):
                        last = pe.transpose((b_ps, c_ps)[h][:, cols(j)], gated_tok[:, j, cols(h)], ident[:, :])
                    last.then_inc(s_gt, 1)

            def mix_out(b):
                pe.wait_ge(s_gated, HALVES * b + HALVES)
                for j in range(TILES):
                    for h in range(HALVES):
                        last = pe.matmul(y_ps[0][:, cols(j)], gated[:, h, cols(j)], wout_sb[:, h, :],
                                         start=(h == 0), stop=(h == HALVES - 1))
                last.then_inc(s_mix, 1)

            def pre(b, s):
                if s == 19:
                    mix_ht(b)
                if s == BACK:
                    mix_in(b)
                if s == BACK + 2:
                    mix_zin(b, 1)
                    mix_xdbl(b)

            def mix(b, s):
                n = s - SCAN
                if s == 0:
                    mix_dtp(b)
                    mix_bn(b, 0)
                    mix_zin(b, 0)
                if s == 2:
                    mix_skip(b)
                    mix_bn(b, 1)
                if 0 <= n < STATE - 2:
                    mix_bn(b, n + 2)
                if s == BACK + 1:
                    mix_gt(b)
                if s == BACK + 2:
                    mix_out(b)

            def late(b, s):
                n = s - SCAN
                if 0 <= n < STATE:
                    mix_cn(b, n)
                if 1 <= n <= STATE:
                    mix_acc(b, n - 1)

            def norm_t(i, t, m):
                p = {2: "a.norm2", 3: "b.norm3"}[m]
                pe.wait_ge(s_ntok[m], t + 1)
                bank_free(pe, i, p)
                for j in range(TILES):
                    last = pe.transpose(work_of(p)[:, cols(j)], n_tok[:, j, :], ident[:, :])
                last.then_inc(*made(p))

            def norm1_t(t):
                pe.wait_ge(s_ntok[1], t + 1)
                pe.wait_ge(s_gated, HALVES * t + HALVES)
                for j in range(TILES):
                    last = pe.transpose(c_ps[:, cols(j)], n_tok[:, j, :], ident[:, :])
                last.then_inc(s_n1, 1)

            def ffn_up(i, c, j):
                p = c + ".up%d" % j
                m = {"a": 1, "c": 3}[c]
                if j == 0:
                    if c == "a":
                        pe.wait_ge(s_n1lo, i)
                    else:
                        evacuated(pe, i - 1, "b.norm3")
                bank_free(pe, i, p)
                pe.matmul(work_of(p)[:, :], up_t[:, cols(j)], n_hi[m][:, :], start=True, stop=False)
                pe.matmul(work_of(p)[:, :], up_t[:, cols(j)], n_lo[m][:, :], start=False, stop=True
                          ).then_inc(*made(p))

            def ffn_down(i, c, part):
                p = c + ".down"
                if part == 0:
                    evacuated(pe, i, c + ".up2")
                    evacuated(pe, i, c + ".up3")
                    bank_free(pe, i, p)
                for k in range(FB):
                    last = pe.matmul(work_of(p)[:, cols(part)], gelu[c][:, k, cols(part)], down_t[:, k, :],
                                     start=(k == 0), stop=(k == FB - 1))
                if part == TILES - 1:
                    last.then_inc(*made(p))

            def ffn_sumsq(i, t, c):
                p = c + ".sumsq"
                pe.wait_ge(s_sqsum[c], 3 * t + 3)
                bank_free(pe, i, p)
                for j in range(TILES):
                    last = pe.matmul(work_of(p)[:, j:j + 1], sq_sum[c][:, cols(j)], ones[:, 0:1],
                                     start=True, stop=True)
                last.then_inc(*made(p))

            def gru_in(i, j):
                p = ("a.in%d" if j < 6 else "b.in%d") % j
                if j == 0:
                    evacuated(pe, i, "a.norm2")
                bank_free(pe, i, p)
                three(work_of(p)[:, :], w12_hi[:, cols(j)], w12_lo[:, cols(j)], n_hi[2][:, :], n_lo[2][:, :]
                      ).then_inc(*made(p))

            def gru_gate(i, t, which, j, k):
                p = "b.%s%d" % (which, j)
                if p == "b.z0":
                    pe.wait_ge(s_inlo, FB * t + k + 1)
                if k == 0:
                    bank_free(pe, i, p)
                at = (which == "h") * FF + j * P
                last = three(work_of(p)[:, :], wzh_hi[:, k, at:at + P], wzh_lo[:, k, at:at + P],
                             in_hi[:, k, :], in_lo[:, k, :], start=(k == 0), stop=(k == FB - 1))
                if k == FB - 1:
                    last.then_inc(*made(p))

            def gru_out(i, t, part):
                p = "b.out"
                if part == 0:
                    pe.wait_ge(s_mixed, FB * t + FB)
                    bank_free(pe, i, p)
                for k in range(FB):
                    last = pe.matmul(work_of(p)[:, cols(part)], mixed[:, k, cols(part)], wo_sb[:, k, :],
                                     start=(k == 0), stop=(k == FB - 1))
                if part == TILES - 1:
                    last.then_inc(*made(p))

            IN_AT = {21: (0, 1), 22: (2, 3, 4, 5)}
            GATES_AT = {3: (("z", 0), ("h", 0)), 4: (("z", 1),), 5: (("h", 1),), 6: (("z", 2),), 7: (("h", 2),),
                        8: (("z", 3),), 10: (("h", 3),)}

            def a(i, t, s):
                if s == 1:
                    norm1_t(t)
                if s == 3:
                    for j in range(FB):
                        ffn_up(i, "a", j)
                if s == 14:
                    ffn_sumsq(i, t, "a")
                if s in (15, 16):
                    ffn_down(i, "a", 2 * (s - 15))
                    ffn_down(i, "a", 2 * (s - 15) + 1)
                if s == 19:
                    norm_t(i, t, 2)
                for j in IN_AT.get(s, ()):
                    gru_in(i, j)

            def b(i, t, s):
                if s == 0:
                    gru_in(i, 6)
                    gru_in(i, 7)
                for which, j in GATES_AT.get(s, ()):
                    for k in range(FB):
                        gru_gate(i, t, which, j, k)
                if s in (13, 14):
                    gru_out(i, t, 2 * (s - 13))
                    gru_out(i, t, 2 * (s - 13) + 1)
                if s == 17:
                    norm_t(i, t, 3)

            def c(i, t, s):
                if s == 2:
                    for j in range(FB):
                        ffn_up(i, "c", j)
                if s == 9:
                    ffn_sumsq(i, t, "c")
                if s in (11, 12):
                    ffn_down(i, "c", 2 * (s - 11))
                    ffn_down(i, "c", 2 * (s - 11) + 1)

            pe.wait_ge(s_const, 3)
            pe.wait_ge(s_eye, 2)
            pe.wait_ge(s_win, 1)
            pe.wait_ge(s_wdt, 1)
            pe.wait_ge(s_pick, 1)
            pe.wait_ge(s_A, 1)
            rounds(pe, pre, mix, a, b, c, prepare, late)


_INS = ["x", "gamma", "beta", "W_in", "W_conv", "b_conv", "W_x", "W_dt", "b_dt", "A_log", "Dskip", "W_out",
        "W1", "b1", "W2", "b2", "Wz", "bz", "Wh", "bh", "Wo", "bo", "w_up", "w_down"]


def kernel(**inputs):
    import numpy as np
    import concourse.bacc as bacc
    from concourse import mybir
    from concourse.bass_utils import run_bass_kernel_spmd

    nc = bacc.Bacc("TRN2", target_bir_lowering=False, num_devices=1)
    short = {}
    for name, a in inputs.items():
        for prefix in ("L0_attn_a_", "L0_attn_b_", "L0_ffn_"):
            if name.startswith(prefix):
                short[name[len(prefix):]] = np.ascontiguousarray(a)
    arrays, args = {}, []
    for name in _INS:
        a = short[name]
        arrays[f"in_{name}"] = a
        args.append(nc.dram_tensor(f"in_{name}", a.shape, mybir.dt.from_np(a.dtype), kind="ExternalInput").ap())
    x = short["x"]
    args.append(nc.dram_tensor("out_x", x.shape, mybir.dt.from_np(x.dtype), kind="ExternalOutput").ap())
    build(nc, *args)
    r = run_bass_kernel_spmd(nc, [arrays], core_ids=[0])
    return r.results[0]["out_x"]
```
